# Optimizing a Trainium2 kernel written in Bass

```python
import numpy as np
import jax
import jax.numpy as jnp

def _softmax(x, axis=-1):
    return jax.nn.softmax(x, axis=axis)

def _gelu(x):
    return jax.nn.gelu(x, approximate=True)

def _silu(x):
    return jax.nn.silu(x)

def _sigmoid(x):
    return jax.nn.sigmoid(x)

def _layernorm(x, axis=-1, eps=1e-05):
    m = jnp.mean(x, axis=axis, keepdims=True)
    v = jnp.var(x, axis=axis, keepdims=True)
    return (x - m) / jnp.sqrt(v + eps)

def _scatter_add(tgt, idx, src, axis=0):
    return tgt.at[idx].add(src)

def _segment_sum(src, seg, n):
    return jax.ops.segment_sum(src, seg, n)
kernel_name = 'mk_gnn_preln_d2_gnn_r8_91cdb6'

def setup_inputs(seed: int=0):
    np.random.seed(seed)
    _w = jnp.asarray

    def _rec_inputs():
        import jax
        import jax.numpy as jnp
        _gk = jax.random.key(seed)
        x = -0.000202 + 1 * jax.random.normal(jax.random.fold_in(_gk, 1), (6250, 128), jnp.float32)
        _s = jax.random.randint(jax.random.fold_in(_gk, 2), (100000,), 0, 6250, jnp.int32)
        _d = jax.random.randint(jax.random.fold_in(_gk, 3), (100000,), 0, 6250, jnp.int32)
        _loop = jnp.arange(6250, dtype=jnp.int32)
        src = jnp.concatenate([_s, _d, _loop])
        dst = jnp.concatenate([_d, _s, _loop])
        _o = jnp.argsort(dst, stable=True)
        src = src[_o]
        dst = dst[_o]
        edge_attr_50 = jax.random.uniform(jax.random.fold_in(_gk, 11), (206250, 50), jnp.float32, 0.0, 1)
        edge_type_3 = jax.random.randint(jax.random.fold_in(_gk, 13), (206250,), 0, 3, jnp.int32)
        node_type_3 = jax.random.randint(jax.random.fold_in(_gk, 14), (6250,), 0, 3, jnp.int32)
        return (x, src, dst, edge_attr_50, edge_type_3, node_type_3)
    x, src, dst, edge_attr_50, edge_type_3, node_type_3 = _rec_inputs()

    def _L0_gnn_setup():
        import jax, jax.numpy as jnp
        import numpy as np
        N = 6250
        E = 100000
        IN_C = 128
        OUT_C = 128
        N_TYPES = 3
        NEG_SLOPE = 0.2
        key = jax.random.key(seed)
        ks = jax.random.split(key, 10)
        x = jax.random.normal(ks[0], (N, IN_C), dtype=jnp.float32)
        edge_index = jax.random.randint(ks[1], (2, E), 0, N, dtype=jnp.int32)
        edge_type = jax.random.randint(ks[2], (E,), 0, N_TYPES, dtype=jnp.int32)
        node_type = jax.random.randint(ks[3], (N,), 0, 3, dtype=jnp.int32)
        s = 1.0 / np.sqrt(IN_C)
        emb_table = jax.random.normal(ks[4], (3, IN_C), dtype=jnp.float32)
        W = jax.random.normal(ks[5], (N_TYPES, IN_C, OUT_C), dtype=jnp.float32) * s
        att_src = jax.random.normal(ks[6], (N_TYPES, OUT_C), dtype=jnp.float32) * s
        att_dst = jax.random.normal(ks[7], (N_TYPES, OUT_C), dtype=jnp.float32) * s
        bias = jax.random.normal(ks[8], (N_TYPES, OUT_C), dtype=jnp.float32) * 0.01
        return {'x': x, 'edge_index': edge_index, 'edge_type': edge_type, 'node_type': node_type, 'emb_table': emb_table, 'W': W, 'att_src': att_src, 'att_dst': att_dst, 'bias': bias}
    _L0_gnn_all = _L0_gnn_setup()
    _L0_gnn_in = {k: v for k, v in _L0_gnn_all.items() if k in ('emb_table', 'W', 'att_src', 'att_dst', 'bias')}
    del _L0_gnn_all

    def _L1_gnn_setup():
        import jax, jax.numpy as jnp
        import numpy as np
        N_NODES = 6250
        N_EDGES = 200000
        HIDDEN = 128
        N_RBF = 50

        def _linear_init(key, fan_in, fan_out):
            kw, kb = jax.random.split(key)
            bound = 1.0 / np.sqrt(fan_in)
            W = jax.random.uniform(kw, (fan_in, fan_out), minval=-bound, maxval=bound, dtype=jnp.float32)
            b = jax.random.uniform(kb, (fan_out,), minval=-bound, maxval=bound, dtype=jnp.float32)
            return (W, b)
        key = jax.random.key(seed)
        ks = jax.random.split(key, 9)
        x = jax.random.normal(ks[0], (N_NODES, HIDDEN), dtype=jnp.float32)
        edge_index = jax.random.randint(ks[1], (2, N_EDGES), 0, N_NODES, dtype=jnp.int32)
        edge_attr = jax.random.uniform(ks[2], (N_EDGES, N_RBF), dtype=jnp.float32)
        fW1, fb1 = _linear_init(ks[3], N_RBF, HIDDEN)
        fW2, fb2 = _linear_init(ks[4], HIDDEN, HIDDEN)
        dW, db = _linear_init(ks[5], HIDDEN, HIDDEN)
        uW1, ub1 = _linear_init(ks[6], HIDDEN, HIDDEN)
        uW2, ub2 = _linear_init(ks[7], HIDDEN, HIDDEN)
        return {'x': x, 'edge_index': edge_index, 'edge_attr': edge_attr, 'fW1': fW1, 'fb1': fb1, 'fW2': fW2, 'fb2': fb2, 'dW': dW, 'db': db, 'uW1': uW1, 'ub1': ub1, 'uW2': uW2, 'ub2': ub2}
    _L1_gnn_all = _L1_gnn_setup()
    _L1_gnn_in = {k: v for k, v in _L1_gnn_all.items() if k in ('fW1', 'fb1', 'fW2', 'fb2', 'dW', 'db', 'uW1', 'ub1', 'uW2', 'ub2')}
    del _L1_gnn_all
    return {'x': x, 'src': src, 'dst': dst, 'edge_attr_50': edge_attr_50, 'edge_type_3': edge_type_3, 'node_type_3': node_type_3, 'L0_gnn_emb_table': _L0_gnn_in['emb_table'], 'L0_gnn_W': _L0_gnn_in['W'], 'L0_gnn_att_src': _L0_gnn_in['att_src'], 'L0_gnn_att_dst': _L0_gnn_in['att_dst'], 'L0_gnn_bias': _L0_gnn_in['bias'], 'L1_gnn_fW1': _L1_gnn_in['fW1'], 'L1_gnn_fb1': _L1_gnn_in['fb1'], 'L1_gnn_fW2': _L1_gnn_in['fW2'], 'L1_gnn_fb2': _L1_gnn_in['fb2'], 'L1_gnn_dW': _L1_gnn_in['dW'], 'L1_gnn_db': _L1_gnn_in['db'], 'L1_gnn_uW1': _L1_gnn_in['uW1'], 'L1_gnn_ub1': _L1_gnn_in['ub1'], 'L1_gnn_uW2': _L1_gnn_in['uW2'], 'L1_gnn_ub2': _L1_gnn_in['ub2']}

def reference(x, src, dst, edge_attr_50, edge_type_3, node_type_3, L0_gnn_emb_table, L0_gnn_W, L0_gnn_att_src, L0_gnn_att_dst, L0_gnn_bias, L1_gnn_fW1, L1_gnn_fb1, L1_gnn_fW2, L1_gnn_fb2, L1_gnn_dW, L1_gnn_db, L1_gnn_uW1, L1_gnn_ub1, L1_gnn_uW2, L1_gnn_ub2):
    import jax
    import jax.numpy as jnp

    def _L0_gnn_ref(x, edge_index, edge_type, node_type, emb_table, W, att_src, att_dst, bias):
        import jax, jax.numpy as jnp
        import numpy as np
        N = 6250
        E = 100000
        IN_C = 128
        OUT_C = 128
        N_TYPES = 3
        NEG_SLOPE = 0.2
        n = x.shape[0]
        x = x + emb_table[node_type]
        src, dst = (edge_index[0], edge_index[1])
        out_sum = jnp.zeros((n, OUT_C), dtype=x.dtype)
        for t in range(N_TYPES):
            xw = x @ W[t]
            a_s = xw @ att_src[t]
            a_d = xw @ att_dst[t]
            mask = edge_type == t
            e_raw = jax.nn.leaky_relu(a_s[src] + a_d[dst], NEG_SLOPE)
            e_self = jax.nn.leaky_relu(a_s + a_d, NEG_SLOPE)
            e_masked = jnp.where(mask, e_raw, -jnp.inf)
            m = jnp.maximum(jax.ops.segment_max(e_masked, dst, num_segments=n), e_self)
            m = jax.lax.stop_gradient(m)
            w_edge = jnp.where(mask, jnp.exp(e_raw - m[dst]), 0.0)
            w_self = jnp.exp(e_self - m)
            denom = jax.ops.segment_sum(w_edge, dst, num_segments=n) + w_self
            num = jax.ops.segment_sum(w_edge[:, None] * xw[src], dst, num_segments=n) + w_self[:, None] * xw
            out_sum = out_sum + num / denom[:, None] + bias[t]
        return out_sum

    def _L1_gnn_ref(x, edge_index, edge_attr, fW1, fb1, fW2, fb2, dW, db, uW1, ub1, uW2, ub2):
        import jax, jax.numpy as jnp
        import numpy as np
        N_NODES = 6250
        N_EDGES = 200000
        HIDDEN = 128
        N_RBF = 50

        def _linear_init(key, fan_in, fan_out):
            kw, kb = jax.random.split(key)
            bound = 1.0 / np.sqrt(fan_in)
            W = jax.random.uniform(kw, (fan_in, fan_out), minval=-bound, maxval=bound, dtype=jnp.float32)
            b = jax.random.uniform(kb, (fan_out,), minval=-bound, maxval=bound, dtype=jnp.float32)
            return (W, b)
        src, dst = (edge_index[0], edge_index[1])
        filters = jax.nn.silu(edge_attr @ fW1 + fb1) @ fW2 + fb2
        messages = (x[src] @ dW + db) * filters
        aggregated = jax.ops.segment_sum(messages, dst, num_segments=x.shape[0])
        upd = jax.nn.silu(aggregated @ uW1 + ub1) @ uW2 + ub2
        return x + upd
    edge_index = jnp.stack([src, dst])
    h = jnp.maximum(_layernorm(x, axis=-1), 0.0)
    x = x + _L0_gnn_ref(h, edge_index, edge_type_3, node_type_3, L0_gnn_emb_table, L0_gnn_W, L0_gnn_att_src, L0_gnn_att_dst, L0_gnn_bias)
    h = jnp.maximum(_layernorm(x, axis=-1), 0.0)
    x = x + _L1_gnn_ref(h, edge_index, edge_attr_50, L1_gnn_fW1, L1_gnn_fb1, L1_gnn_fW2, L1_gnn_fb2, L1_gnn_dW, L1_gnn_db, L1_gnn_uW1, L1_gnn_ub1, L1_gnn_uW2, L1_gnn_ub2)
    return x

_drawn_inputs = setup_inputs


def setup_inputs(seed=0):
    import zlib

    import numpy as np

    out = dict(_drawn_inputs(seed))
    spreads = {}
    factors = {'edge_attr_50': 5.857,
     'L0_gnn_bias': 5.754,
     'L1_gnn_db': 5.845,
     'L1_gnn_ub1': 8.0,
     'L1_gnn_ub2': 3.478}
    for name, (base, spread) in spreads.items():
        noise = np.random.default_rng([zlib.crc32(name.encode()), seed]).standard_normal(out[name].shape)
        drawn = base * np.exp(spread * noise) if base else spread * noise
        out[name] = jnp.asarray(drawn.astype(out[name].dtype))
    for name, factor in factors.items():
        out[name] = (out[name] * factor).astype(out[name].dtype)
    return out
```

```python
import numpy as np
import concourse.bass as bass
from concourse import mybir
from contextlib import ExitStack

N, D, NT, RBF = 6250, 128, 3, 50
E = 206250
P = 128
CH = 6
UE = CH * P
SL = 6
NU = -(-E // (UE * SL)) * SL
TURNS = NU // SL
EP = NU * UE
W = 32
KEYS = NT * W
G = 7
TILES = -(-N // P)
GROUPS = TILES // G
GN = G * P
NP = TILES * P
NW = NP + W
PASSES = NP // W
ROW = 132
TQ = NU // 3
SLOPE = 0.2
EPS = 1e-5
BIG = 1e30
assert TILES % G == 0 and TQ <= P and GN // 2 <= 512

fp32, bf16 = mybir.dt.float32, mybir.dt.bfloat16
i32, u16 = mybir.dt.int32, mybir.dt.uint16
ALU, ACT, AX = mybir.AluOpType, mybir.ActivationFunctionType, mybir.AxisListType


def gather(eng, out, table, idx, done):
    eng.indirect_dma_start(out=out, out_offset=None, in_=table[:, :],
                           in_offset=bass.IndirectOffsetOnAxis(ap=idx, axis=0)).then_inc(done, 16)


class Held:

    def __init__(self, nc, ctx):
        sb = lambda name, shape, dt=fp32: ctx.enter_context(nc.sbuf_tensor(name, shape, dt))
        self.cst = sb("cst", [P, 7 * P + KEYS])
        c = self.cst
        self.ident = c[:, 0:P]
        self.ones = c[:, P:2 * P]
        self.sel_pos = c[:, 2 * P:3 * P]
        self.sel_neg = c[:, 3 * P:4 * P]
        self.sel_gap = c[:, 4 * P:5 * P]
        self.sel_den = c[:, 5 * P:6 * P]
        self.iota = c[:, 7 * P:7 * P + KEYS]
        self.dst = sb("dst", [P, NU, CH], u16)
        self.typ = sb("typ", [P, NU, CH], bf16)
        self.key = sb("key", [P, NU, CH], bf16)
        self.ubase = sb("ubase", [P, NU])
        self.base = sb("base", [P, NU])
        self.base_i = sb("base_i", [P, NU], i32)
        self.wide = sb("wide", [P, 1])
        self.narrow = sb("narrow", [P, 1])
        self.passes = sb("passes", [P, 1], i32)
        self.sweep = sb("sweep", [P, 1])


def constants():
    c = np.zeros((P, 7 * P + KEYS), np.float32)
    c[:, 0:P] = np.eye(P)
    c[:, P:2 * P] = 1
    c[0, 2 * P:3 * P] = 1
    c[32, 2 * P:3 * P] = -1
    c[0, 3 * P:4 * P] = SLOPE
    c[32, 3 * P:4 * P] = -1
    c[32, 4 * P:5 * P] = 1
    c[64, 5 * P:6 * P] = 1
    c[:, 7 * P:] = np.arange(KEYS)
    return c


def prepare_edges(nc, h, a):
    with ExitStack() as ctx:
        dst_i = ctx.enter_context(nc.sbuf_tensor("dst_i", [P, NU, CH], i32))
        typ_i = ctx.enter_context(nc.sbuf_tensor("typ_i", [P, NU, CH], i32))
        lim = ctx.enter_context(nc.sbuf_tensor("lim", [P, 2, NU], fp32))
        col = ctx.enter_context(nc.sbuf_tensor("col", [P, 2, 3], fp32))
        span = ctx.enter_context(nc.sbuf_tensor("span", [P, NU], fp32))
        top = ctx.enter_context(nc.sbuf_tensor("top", [P, 1], fp32))
        ps_t = [ctx.enter_context(nc.psum_tensor(f"ps_t{k}", [P, 512], fp32)) for k in range(2)]
        ps_b = [ctx.enter_context(nc.psum_tensor(f"ps_b{k}", [P, 512], fp32)) for k in range(2)]
        sem = lambda name: ctx.enter_context(nc.semaphore("pe_" + name))
        cst_in, dst_in, typ_in = sem("cst_in"), sem("dst_in"), sem("typ_in")
        lims, turned, cols, spread, steps = sem("lims"), sem("turned"), sem("cols"), sem("spread"), sem("steps")
        block = ctx.enter_context(nc.Block())

        @block.sync
        def _(sp):
            sp.dma_start(h.cst[:, :], a["cst"][:, :]).then_inc(cst_in, 16)
            sp.dma_start(dst_i[:, :, :], a["dst"][:, :, :]).then_inc(dst_in, 16)
            sp.dma_start(typ_i[:, :, :], a["edge_type_3"][:, :, :]).then_inc(typ_in, 16)

        @block.vector
        def _(dve):
            nc.vector.memset(h.sweep[:, :], 0.0)
            dve.wait_ge(dst_in, 16)
            nc.vector.tensor_reduce(out=lim[:, 0, :], in_=dst_i[:, :, :], op=ALU.min, axis=AX.X)
            nc.vector.tensor_reduce(out=lim[:, 1, :], in_=dst_i[:, :, :], op=ALU.max, axis=AX.X).then_inc(lims, 1)
            nc.vector.tensor_copy(h.dst[:, :, :], dst_i[:, :, :])
            dve.wait_ge(typ_in, 16)
            nc.vector.tensor_copy(h.typ[:, :, :], typ_i[:, :, :])
            dve.wait_ge(turned, 1)
            for k, op in enumerate((ALU.min, ALU.max)):
                nc.vector.tensor_reduce(out=col[0:TQ, k, :], in_=ps_t[k][0:TQ, 0:3 * P].rearrange("u (q p) -> u q p", q=3),
                                        op=op, axis=AX.X).then_inc(cols, 1)
            dve.wait_ge(spread, 1)
            nc.vector.tensor_copy(h.ubase[:, :], ps_b[0][:, 0:NU]).then_inc(steps, 1)
            dve.wait_ge(steps, 1)
            nc.vector.tensor_tensor(span[:, :], ps_b[1][:, 0:NU], h.ubase[:, :], ALU.subtract).then_inc(steps, 1)
            dve.wait_ge(steps, 2)
            nc.vector.tensor_reduce(out=top[:, :], in_=span[:, :], op=ALU.max, axis=AX.X).then_inc(steps, 1)
            dve.wait_ge(steps, 3)
            nc.vector.tensor_scalar(h.wide[:, :], top[:, :], W - 0.5, None, ALU.is_gt).then_inc(steps, 1)
            dve.wait_ge(steps, 4)
            nc.vector.tensor_scalar(h.narrow[:, :], h.wide[:, :], -1.0, 1.0, ALU.mult, ALU.add)
            nc.vector.tensor_scalar(h.passes[:, :], h.wide[:, :], PASSES - 1.0, 1.0, ALU.mult, ALU.add)

        @block.tensor
        def _(pe):
            pe.wait_ge(cst_in, 16)
            pe.wait_ge(lims, 1)
            for k in range(2):
                for q in range(3):
                    last = nc.tensor.transpose(ps_t[k][0:TQ, q * P:(q + 1) * P], lim[:, k, q * TQ:(q + 1) * TQ], h.ident)
            last.then_inc(turned, 1)
            pe.wait_ge(cols, 2)
            for k in range(2):
                for q in range(3):
                    last = nc.tensor.matmul(ps_b[k][:, q * TQ:(q + 1) * TQ],
                                            col[0:TQ, k, q:q + 1].to_broadcast([TQ, P]), h.ident[0:TQ, 0:TQ],
                                            start=True, stop=True)
            last.then_inc(spread, 1)


def prepare_nodes(nc, h, a, acc, state, table):
    with ExitStack() as ctx:
        sb = lambda name, shape, dt=fp32: ctx.enter_context(nc.sbuf_tensor("pn_" + name, shape, dt))
        pb = lambda name: ctx.enter_context(nc.psum_tensor("pn_" + name, [P, 1024], fp32))
        sem = lambda name: ctx.enter_context(nc.semaphore("pn_" + name))
        wt, att, emb = sb("wt", [P, NT, D]), sb("att", [P, 2 * NT]), sb("emb", [3, D])
        score = sb("score", [P, 2 * NT])
        rows_w = sb("rows_w", [P, NT, 96])
        nt_i, nt1h = sb("nt_i", [3, GN], i32), sb("nt1h", [3, GN])
        kind = sb("kind", [P, 1])
        kind_i = sb("kind_i", [P, 1], i32)
        x, xc, sq = sb("x", [P, G, D]), sb("xc", [P, G, D]), sb("sq", [P, G, D])
        mean, var = sb("mean", [P, G]), sb("var", [P, G])
        dev, inv = sb("dev", [P, G]), sb("inv", [P, G])
        rows = sb("rows", [P, G, ROW])
        xt = sb("xt", [P, GN])
        ps_e, ps_x, ps_r = pb("ps_e"), pb("ps_x"), pb("ps_r")
        ps_s = ctx.enter_context(nc.psum_tensor("ps_s", [P, 512], fp32))
        w_in, att_in, emb_in, x_in, nt_in, out_done = sem("w_in"), sem("att_in"), sem("emb_in"), sem("x_in"), sem("nt_in"), sem("out_done")
        sc_ps, sc_ok, x_used, nt_used, onehot, emb_ok = sem("sc_ps"), sem("sc_ok"), sem("x_used"), sem("nt_used"), sem("onehot"), sem("emb_ok")
        n_sum, n_mean, n_cen, n_sq, n_var, n_dev, n_inv = (sem(f"n_{k}") for k in ("sum", "mean", "cen", "sq", "var", "dev", "inv"))
        n_nrm, feat, xt_ps, xt_ok, as_ps, as_ok = sem("n_nrm"), sem("feat"), sem("xt_ps"), sem("xt_ok"), sem("as_ps"), sem("as_ok")
        row_ps, row_out, m_ok, acc_ok, cleared, prep = sem("row_ps"), sem("row_out"), sem("m_ok"), sem("acc_ok"), sem("cleared"), sem("prep")
        eps = sb("eps", [P, 1])
        epsilon, rows_free = sem("epsilon"), sem("rows_free")
        block = ctx.enter_context(nc.Block())

        @block.sync
        def _(sp):
            sp.sem_inc(rows_free, 1)
            sp.dma_start(wt[:, :, :], a["w_t"][:, :, :]).then_inc(w_in, 16)
            sp.dma_start(att[:, :], a["att"][:, :]).then_inc(att_in, 16)
            sp.dma_start(emb[:, :], a["L0_gnn_emb_table"][:, :]).then_inc(emb_in, 16)
            sp.dma_start(x[:, :, :], a["x"][0, :, :, :]).then_inc(x_in, 16)
            sp.dma_start(nt_i[:, :], a["node_type_3"][0:1, 0:GN].to_broadcast([3, GN])).then_inc(nt_in, 16)
            with sp.Fori(0, GROUPS - 1) as g:
                sp.wait_ge(x_used, g + 1)
                sp.dma_start(x[:, :, :], a["x"][bass.ds(g + 1, 1), :, :, :].rearrange("o p t f -> (o p) t f")).then_inc(x_in, 16)
                sp.wait_ge(onehot, g + 1)
                sp.dma_start(nt_i[:, :], a["node_type_3"][0:1, bass.ds((g + 1) * GN, GN)].to_broadcast([3, GN])).then_inc(nt_in, 16)
                sp.wait_ge(feat, g + 1)
                sp.wait_ge(as_ok, g + 1)
                sp.dma_start(table[bass.ds(g * GN, GN), :].rearrange("(t p) r -> p t r", p=P), rows[:, :, :]).then_inc(out_done, 16)
                sp.wait_ge(out_done, 16 * g + 16)
                sp.sem_inc(rows_free, 1)
            sp.wait_ge(feat, GROUPS)
            sp.wait_ge(as_ok, GROUPS)
            sp.dma_start(table[(GROUPS - 1) * GN:GROUPS * GN, :].rearrange("(t p) r -> p t r", p=P), rows[:, :, :]).then_inc(out_done, 16)
            sp.wait_ge(out_done, 16 * GROUPS)

        @block.gpsimd
        def _(pool):
            pool.sem_inc(acc_ok, 1)
            pool.iota(kind_i[:, :], pattern=[[0, 1]], base=0, channel_multiplier=1).then_inc(prep, 1)
            pool.wait_ge(prep, 1)
            pool.tensor_copy(kind[:, :], kind_i[:, :]).then_inc(prep, 1)
            for k, (part, value) in enumerate(((state[64:P, :, :], 1.0), (state[0:64, :, NP:NW], 0.0), (acc[:, :, NP:NW], 0.0))):
                pool.wait_ge(prep, k + 2)
                pool.memset(part, value).then_inc(prep, 1)
            pool.wait_ge(prep, 5)
            with pool.Fori(0, GROUPS) as g:
                pool.wait_ge(xt_ok, g + 1)
                for t in range(NT):
                    last = pool.tensor_copy(acc[:, t, bass.ds(g * GN, GN)], xt[:, :])
                last.then_inc(acc_ok, 1)

        @block.tensor
        def _(pe):
            pe.wait_ge(w_in, 16)
            pe.wait_ge(att_in, 16)
            for t in range(NT):
                for k in range(2):
                    c = k * NT + t
                    last = nc.tensor.matmul(ps_s[:, c:c + 1], wt[:, t, :], att[:, c:c + 1], start=True, stop=True)
            last.then_inc(sc_ps, 1)
            pe.wait_ge(emb_in, 16)
            pe.wait_ge(sc_ok, 2)
            with pe.Fori(0, GROUPS) as g:
                pe.wait_ge(onehot, g + 1)
                for t in range(G):
                    last = nc.tensor.matmul(ps_e[:, t * P:(t + 1) * P], nt1h[:, t * P:(t + 1) * P], emb[:, :], start=True, stop=True)
                last.then_inc(emb_ok, 1)
                pe.wait_ge(feat, g + 1)
                for t in range(G):
                    last = nc.tensor.transpose(ps_x[:, t * P:(t + 1) * P], rows[:, t, 0:D], h.ident)
                last.then_inc(xt_ps, 1)
                pe.wait_ge(xt_ok, g + 1)
                for t in range(G):
                    last = nc.tensor.matmul(ps_s[:, 8 + NT * t:8 + NT * t + NT], xt[:, t * P:(t + 1) * P], score[:, 0:NT], start=True, stop=True)
                last.then_inc(as_ps, 1)
                for t in range(NT):
                    pe.wait_ge(row_out, g * NT + t + 1)
                    for k in range(2):
                        last = nc.tensor.matmul(ps_r[0:96, k * 512:k * 512 + GN // 2], rows_w[:, t, :],
                                                xt[:, k * GN // 2:(k + 1) * GN // 2], start=True, stop=True)
                    last.then_inc(row_ps, 1)

        @block.scalar
        def _(act):
            act.wait_ge(epsilon, 1)
            act.sem_inc(row_out, 1)
            with act.Fori(0, GROUPS) as g:
                act.wait_ge(n_var, g + 1)
                nc.scalar.activation(dev[:, :], var[:, :], ACT.Sqrt, bias=eps[:, :], scale=1.0 / D).then_inc(n_dev, 1)
                for t in range(NT):
                    act.wait_ge(row_ps, g * NT + t + 1)
                    nc.scalar.copy(state[0:64, t, bass.ds(g * GN, GN)].rearrange("p (k n) -> p k n", k=2),
                                   ps_r[0:64, :].rearrange("p (k n) -> p k n", k=2)[:, :, 0:GN // 2]).then_inc(row_out, 1)

        @block.vector
        def _(dve):
            nc.vector.memset(eps[:, :], EPS).then_inc(epsilon, 1)
            nc.vector.memset(rows[:, :, D + NT:ROW], 0.0)
            nc.vector.memset(rows_w[:, :, :], 0.0).then_inc(sc_ok, 1)
            dve.wait_ge(sc_ps, 1)
            nc.vector.tensor_copy(score[:, :], ps_s[:, 0:2 * NT]).then_inc(n_cen, 1)
            dve.wait_ge(n_cen, 1)
            dve.wait_ge(sc_ok, 1)
            nc.vector.tensor_copy(rows_w[:, :, 0], score[:, NT:2 * NT])
            nc.vector.tensor_tensor(rows_w[:, :, 32], score[:, 0:NT], score[:, NT:2 * NT], ALU.add).then_inc(sc_ok, 1)
            dve.wait_ge(prep, 2)
            with dve.Fori(0, GROUPS) as g:
                dve.wait_ge(nt_in, 16 * g + 16)
                nc.vector.tensor_scalar(nt1h[:, :], nt_i[:, :], kind[0:3, :], None, ALU.is_equal).then_inc(onehot, 1)
                dve.wait_ge(x_in, 16 * g + 16)
                nc.vector.tensor_reduce(out=mean[:, :], in_=x[:, :, :], op=ALU.add, axis=AX.X).then_inc(n_sum, 1)
                dve.wait_ge(n_sum, g + 1)
                nc.vector.tensor_scalar(mean[:, :], mean[:, :], 1.0 / D, None, ALU.mult).then_inc(n_mean, 1)
                dve.wait_ge(n_mean, g + 1)
                nc.vector.tensor_tensor(xc[:, :, :], x[:, :, :], mean[:, :].unsqueeze(2).to_broadcast([P, G, D]), ALU.subtract).then_inc(x_used, 1)
                dve.wait_ge(x_used, g + 1)
                nc.vector.tensor_tensor(sq[:, :, :], xc[:, :, :], xc[:, :, :], ALU.mult).then_inc(n_sq, 1)
                dve.wait_ge(n_sq, g + 1)
                nc.vector.tensor_reduce(out=var[:, :], in_=sq[:, :, :], op=ALU.add, axis=AX.X).then_inc(n_var, 1)
                dve.wait_ge(n_dev, g + 1)
                nc.vector.reciprocal(inv[:, :], dev[:, :]).then_inc(n_inv, 1)
                dve.wait_ge(n_inv, g + 1)
                nc.vector.tensor_tensor(xc[:, :, :], xc[:, :, :], inv[:, :].unsqueeze(2).to_broadcast([P, G, D]), ALU.mult).then_inc(n_nrm, 1)
                dve.wait_ge(n_nrm, g + 1)
                dve.wait_ge(emb_ok, g + 1)
                dve.wait_ge(rows_free, g + 1)
                nc.vector.scalar_tensor_tensor(out=rows[:, :, 0:D], in0=xc[:, :, :], scalar=0.0,
                                               in1=ps_e[:, 0:GN].rearrange("p (t f) -> p t f", t=G),
                                               op0=ALU.max, op1=ALU.add).then_inc(feat, 1)
                dve.wait_ge(xt_ps, g + 1)
                dve.wait_ge(acc_ok, g + 1)
                nc.vector.tensor_copy(xt[:, :], ps_x[:, 0:GN]).then_inc(xt_ok, 1)
                dve.wait_ge(as_ps, g + 1)
                nc.vector.tensor_copy(rows[:, :, D:D + NT], ps_s[:, 8:8 + NT * G].rearrange("p (t k) -> p t k", k=NT)).then_inc(as_ok, 1)
                dve.wait_ge(row_out, NT * g + NT + 1)
                nc.vector.scalar_tensor_tensor(out=state[32:64, :, bass.ds(g * GN, GN)], in0=state[32:64, :, bass.ds(g * GN, GN)],
                                               scalar=SLOPE, in1=state[32:64, :, bass.ds(g * GN, GN)],
                                               op0=ALU.mult, op1=ALU.max).then_inc(m_ok, 1)


STEPS = 8


def start_pass(nc, dve, h, r, steps, key_ready, begun, rel, with_type):
    done = [0]

    def link(ins):
        done[0] += 1
        ins.then_inc(steps, 1)
        dve.wait_ge(steps, r * STEPS + done[0])

    link(nc.vector.tensor_tensor(h.base[:, :], h.ubase[:, :], h.narrow[:, :].to_broadcast([P, NU]), ALU.mult))
    link(nc.vector.tensor_tensor(h.base[:, :], h.base[:, :], h.sweep[:, :].to_broadcast([P, NU]), ALU.add))
    nc.vector.tensor_copy(h.base_i[:, :], h.base[:, :])
    link(nc.vector.tensor_tensor(rel, h.dst[:, :, :], h.base[:, :].unsqueeze(2).to_broadcast([P, NU, CH]), ALU.subtract))
    link(nc.vector.scalar_tensor_tensor(out=h.sweep[:, :], in0=h.wide[:, :], scalar=float(W), in1=h.sweep[:, :], op0=ALU.mult, op1=ALU.add))
    link(nc.vector.tensor_scalar(h.key[:, :, :], rel, -0.5, None, ALU.is_gt))
    link(nc.vector.scalar_tensor_tensor(out=h.key[:, :, :], in0=rel, scalar=W - 0.5, in1=h.key[:, :, :], op0=ALU.is_lt, op1=ALU.mult))
    if with_type:
        link(nc.vector.scalar_tensor_tensor(out=rel, in0=h.typ[:, :, :], scalar=float(W), in1=rel, op0=ALU.mult, op1=ALU.add))
    link(nc.vector.scalar_tensor_tensor(out=rel, in0=rel, scalar=1.0, in1=h.key[:, :, :], op0=ALU.add, op1=ALU.mult))
    if not with_type:
        done[0] += 1
        dve.sem_inc(steps, 1)
    assert done[0] == STEPS
    nc.vector.tensor_scalar(h.key[:, :, :], rel, -1.0, None, ALU.add).then_inc(key_ready, 1)
    dve.wait_ge(key_ready, r + 1)
    dve.sem_inc(begun, 1)


def pass_count(eng, h):
    return eng.value_load(h.passes[0:1, 0:1], min_val=1, max_val=PASSES)


def bases(nc, engine, h, first, count):
    return nc.values_load_multi_w_load_instructions(h.base_i[0:1, bass.ds(first, count)], engines=[engine],
                                                    min_val=0, max_val=N)[1]


def turns(eng, body):
    body(0, True)
    with eng.Fori(1, TURNS) as i:
        body(i, False)


def load_indices(sp, a, h, idx, idx_in, gathered, landed, also=lambda r, i, s: None):
    for s in range(SL):
        sp.dma_start(idx[s][:, :], a["src"][s, :, :]).then_inc(idx_in[s], 16)
    passes = pass_count(sp, h)
    with sp.Fori(0, passes) as r:
        with sp.Fori(0, TURNS - 1) as i:
            for s in range(SL):
                also(r, i, s)
                sp.wait_ge(gathered[s % XS], GI * (PER * (r * TURNS + i) + s // XS + 1))
                sp.dma_start(idx[s][:, :], a["src"][bass.ds((i + 1) * SL + s, 1), :, :].rearrange("o p c -> (o p) c")).then_inc(idx_in[s], 16)
        for s in range(SL):
            also(r, TURNS - 1, s)
            sp.wait_ge(gathered[s % XS], GI * (PER * (r * TURNS + TURNS - 1) + s // XS + 1))
            sp.dma_start(idx[s][:, :], a["src"][s, :, :]).then_inc(idx_in[s], 16)
    for s in range(SL):
        sp.wait_ge(idx_in[s], 16 * (passes * TURNS + 1))
    sp.sem_inc(landed, 1)


def gather_units(pool, h, table, xg, width, idx, idx_in, gathered, xg_free, pool_turn):
    with pool.Fori(0, pass_count(pool, h)) as r:
        with pool.Fori(0, TURNS) as i:
            for s in range(SL):
                pool.wait_ge(idx_in[s], 16 * (r * TURNS + i + 1))
                pool.wait_ge(xg_free, (r * TURNS + i) * SL + s + 1)
                pool.sem_inc(pool_turn, 1)
                for c in range(CH):
                    gather(pool, xg[:, s % XS, c, 0:width], table, idx[s][:, c:c + 1], gathered[s % XS])


XS = 3
PER = SL // XS
GI = 16 * CH


def attention_edges(nc, h, a, acc, state, table):
    with ExitStack() as ctx:
        sb = lambda name, shape, dt=fp32: ctx.enter_context(nc.sbuf_tensor("ae_" + name, shape, dt))
        pb = lambda name: ctx.enter_context(nc.psum_tensor("ae_" + name, [P, 512], fp32))
        sem = lambda name: ctx.enter_context(nc.semaphore("ae_" + name))
        idx = [sb(f"idx{s}", [P, CH], i32) for s in range(SL)]
        xg = sb("xg", [P, XS, CH, ROW])
        oh3, pick = sb("oh3", [P, CH, NT], bf16), sb("pick", [P, CH, NT])
        sc1, sc2 = sb("sc1", [P, 2, CH]), sb("sc2", [P, 2, CH])
        off = sb("off", [P, 2, CH, KEYS], bf16)
        masked = sb("masked", [P, CH, KEYS])
        high, high_k = sb("high", [P, KEYS]), sb("high_k", [KEYS, 1])
        z, lift, drop, gap = (sb(k, [64, KEYS]) for k in ("z", "lift", "drop", "gap"))
        e = sb("e", [P, 2, 2, CH * KEYS])
        e1, e2 = (e[:, k, :, :].rearrange("p b (c k) -> p b c k", c=CH) for k in range(2))
        wgt = e2
        rescale = sb("rescale", [P, 2, KEYS])
        rel = e[:, :, :, :].rearrange("p a b k -> p (a b k)")[:, 0:NU * CH].rearrange("p (u c) -> p u c", c=CH)
        ps_t, ps_z = pb("ps_t"), pb("ps_z")
        ps_c, ps_a, ps_d = ([pb(f"ps_{k}{b}") for b in range(2)] for k in "cad")
        idx_in = [sem(f"idx_in{s}") for s in range(SL)]
        sem_landed = sem("landed")
        gathered = [sem(f"gathered{s}") for s in range(XS)]
        xg_free, pool_turn, steps, key_ready, begun, gap_zero = (sem(k) for k in ("xg_free", "pool_turn", "steps", "key_ready", "begun", "gap_zero"))
        (s_oh, s_pick, s_score, s_off, s_masked, s_high, s_turned, s_highk, s_z, s_zc, s_lift, s_drop, s_gap, s_max,
         s_c, s_e, s_x, s_wgt, s_sum, s_scaled, s_dscaled, s_acc, s_den) = (sem("s_" + k) for k in (
             "oh pick score off masked high turned highk z zc lift drop gap max c e x wgt sum scaled dscaled acc den").split())
        block = ctx.enter_context(nc.Block())

        def kv(ap):
            return ap.rearrange("p (t n) -> p t n", t=NT)

        @block.sync
        def _(sp):
            load_indices(sp, a, h, idx, idx_in, gathered, sem_landed)

        @block.gpsimd
        def _(pool):
            gather_units(pool, h, table, xg, ROW, idx, idx_in, gathered, xg_free, pool_turn)

        @block.scalar
        def _(act):
            with act.Fori(0, pass_count(act, h)) as r:
                def turn(i, first):
                    for s in range(SL):
                        n, b = (r * TURNS + i) * SL + s + 1, s % 2
                        act.wait_ge(s_c, n)
                        nc.scalar.activation(rescale[:, b, :], ps_c[b][:, 2 * KEYS:3 * KEYS], ACT.Exp)
                        if not (first and s < 2):
                            act.wait_ge(s_sum, n - 2)
                        for c in range(CH):
                            nc.scalar.activation(e1[:, b, c, :], ps_c[b][:, 0:KEYS], ACT.Exp, bias=sc1[:, b, c:c + 1])
                            last = nc.scalar.activation(e2[:, b, c, :], ps_c[b][:, KEYS:2 * KEYS], ACT.Exp, bias=sc2[:, b, c:c + 1])
                        last.then_inc(s_e, 1)
                turns(act, turn)

        @block.tensor
        def _(pe):
            pe.sem_inc(xg_free, XS)
            pe.wait_ge(gap_zero, 1)
            with pe.Fori(0, pass_count(pe, h)) as r:
                def sums(n, s):
                    b = s % 2
                    pe.wait_ge(s_wgt, n)
                    for c in range(CH):
                        last = nc.tensor.matmul(ps_a[b][:, 0:KEYS], xg[:, s % XS, c, 0:D], wgt[:, b, c, :], start=(c == 0), stop=(c == CH - 1))
                    last.then_inc(xg_free, 1)
                    for c in range(CH):
                        last = nc.tensor.matmul(ps_d[b][:, 0:KEYS], h.ones, wgt[:, b, c, :], start=(c == 0), stop=(c == CH - 1))
                    last.then_inc(s_sum, 1)

                def turn(i, first):
                    base = bases(nc, mybir.EngineType.PE, h, i * SL, SL)
                    for s in range(SL):
                        n, b = (r * TURNS + i) * SL + s + 1, s % 2
                        pe.wait_ge(s_high, n)
                        nc.tensor.transpose(ps_t[0:KEYS, 0:P], high[:, :], h.ident).then_inc(s_turned, 1)
                        pe.wait_ge(s_highk, n)
                        nc.tensor.matmul(ps_z[:, 0:KEYS], high_k[:, :].to_broadcast([KEYS, P]), h.ident[0:KEYS, 0:KEYS], start=True, stop=False)
                        nc.tensor.matmul(kv(ps_z[:, 0:KEYS]), h.ones[0:1, :], state[0:1, :, bass.ds(base[s], W)], start=False, stop=True).then_inc(s_z, 1)
                        pe.wait_ge(s_max, n)
                        nc.tensor.matmul(ps_c[b][:, 2 * KEYS:3 * KEYS], h.sel_gap[0:64, :], gap[:, :], start=True, stop=True)
                        nc.tensor.matmul(kv(ps_c[b][:, 0:KEYS]), h.sel_pos[0:64, :], state[0:64, :, bass.ds(base[s], W)], start=True, stop=True)
                        nc.tensor.matmul(kv(ps_c[b][:, KEYS:2 * KEYS]), h.sel_neg[0:64, :], state[0:64, :, bass.ds(base[s], W)], start=True, stop=True).then_inc(s_c, 1)
                        if not (first and s < 1):
                            sums(n - 1, (s - 1) % SL)
                pe.wait_ge(key_ready, r + 1)
                pe.sem_inc(begun, 1)
                turns(pe, turn)
                sums((r + 1) * NU, SL - 1)

        @block.vector
        def _(dve):
            nc.vector.memset(gap[:, :], 0.0).then_inc(gap_zero, 1)
            with dve.Fori(0, pass_count(dve, h)) as r:
                def merge_scale(n, s, base, fresh):
                    b = s % 2
                    win = bass.ds(base, W)
                    dve.wait_ge(s_sum, n)
                    if not fresh:
                        dve.wait_ge(s_acc, n - 1)
                        dve.wait_ge(s_den, n - 1)
                    nc.vector.tensor_tensor(acc[:, :, win], acc[:, :, win], kv(rescale[:, b, :]), ALU.mult).then_inc(s_scaled, 1)
                    nc.vector.tensor_tensor(state[64:65, :, win], state[64:65, :, win], kv(rescale[64:65, b, :]), ALU.mult).then_inc(s_dscaled, 1)

                def merge_add(n, s, base):
                    b = s % 2
                    win = bass.ds(base, W)
                    dve.wait_ge(s_scaled, n)
                    nc.vector.tensor_tensor(acc[:, :, win], acc[:, :, win], kv(ps_a[b][:, 0:KEYS]), ALU.add).then_inc(s_acc, 1)
                    dve.wait_ge(s_dscaled, n)
                    nc.vector.tensor_tensor(state[64:65, :, win], state[64:65, :, win], kv(ps_d[b][64:65, 0:KEYS]), ALU.add).then_inc(s_den, 1)

                def larger(n, s):
                    b = s % 2
                    dve.wait_ge(s_e, n)
                    nc.vector.tensor_tensor(e1[:, b, :, :], e1[:, b, :, :], e2[:, b, :, :], ALU.max).then_inc(s_x, 1)

                def weights(n, s):
                    b = s % 2
                    dve.wait_ge(s_x, n)
                    nc.vector.scalar_tensor_tensor(out=wgt[:, b, :, :].rearrange("p c k -> p (c k)"), in0=off[:, b, :, :].rearrange("p c k -> p (c k)"), scalar=0.0,
                                                   in1=e1[:, b, :, :].rearrange("p c k -> p (c k)"), op0=ALU.is_equal, op1=ALU.min).then_inc(s_wgt, 1)

                def turn(i, first):
                    back = 0 if first else 2
                    base = bases(nc, mybir.EngineType.DVE, h, i * SL - back, SL + back)
                    for s in range(SL):
                        n, b = (r * TURNS + i) * SL + s + 1, s % 2
                        lag1, lag2 = not (first and s < 1), not (first and s < 2)
                        unit = i * SL + s
                        before = base[s + back - 2] if lag2 else None
                        now = base[s + back]
                        keys = h.key[:, bass.ds(unit, 1), :].rearrange("p o c -> p (o c)")
                        types = h.typ[:, bass.ds(unit, 1), :].rearrange("p o c -> p (o c)")
                        nc.vector.tensor_tensor(oh3[:, :, :], types.unsqueeze(2).to_broadcast([P, CH, NT]),
                                                h.iota[:, 0:NT].unsqueeze(1).to_broadcast([P, CH, NT]), ALU.is_equal).then_inc(s_oh, 1)
                        nc.vector.tensor_tensor(off[:, b, :, :], h.iota.unsqueeze(1).to_broadcast([P, CH, KEYS]),
                                                keys.unsqueeze(2).to_broadcast([P, CH, KEYS]), ALU.not_equal).then_inc(s_off, 1)
                        dve.wait_ge(s_oh, n)
                        dve.wait_ge(gathered[s % XS], GI * (PER * (r * TURNS + i) + s // XS + 1))
                        nc.vector.tensor_tensor(pick[:, :, :], oh3[:, :, :], xg[:, s % XS, :, D:D + NT], ALU.mult).then_inc(s_pick, 1)
                        if lag2:
                            merge_scale(n - 2, s, before, first and s == 2)
                        dve.wait_ge(s_pick, n)
                        nc.vector.tensor_reduce(out=sc1[:, b, :], in_=pick[:, :, :], op=ALU.add, axis=AX.X).then_inc(s_score, 1)
                        if lag2:
                            merge_add(n - 2, s, before)
                        dve.wait_ge(s_score, n)
                        nc.vector.tensor_scalar(sc2[:, b, :], sc1[:, b, :], SLOPE, None, ALU.mult)
                        dve.wait_ge(s_off, n)
                        nc.vector.scalar_tensor_tensor(out=masked[:, :, :], in0=off[:, b, :, :], scalar=-BIG,
                                                       in1=sc1[:, b, :].unsqueeze(2).to_broadcast([P, CH, KEYS]), op0=ALU.mult, op1=ALU.add).then_inc(s_masked, 1)
                        dve.wait_ge(s_masked, n)
                        nc.vector.tensor_reduce(out=high[:, :], in_=masked[:, :, :].rearrange("p c k -> p k c"), op=ALU.max, axis=AX.X).then_inc(s_high, 1)
                        if lag1:
                            larger(n - 1, s - 1)
                        dve.wait_ge(s_turned, n)
                        nc.vector.tensor_reduce(out=high_k[:, :], in_=ps_t[0:KEYS, 0:P], op=ALU.max, axis=AX.X).then_inc(s_highk, 1)
                        if lag1:
                            weights(n - 1, s - 1)
                        dve.wait_ge(s_z, n)
                        nc.vector.tensor_copy(z[32:33, :], ps_z[32:33, 0:KEYS]).then_inc(s_zc, 1)
                        dve.wait_ge(s_zc, n)
                        nc.vector.scalar_tensor_tensor(out=lift[32:33, :], in0=z[32:33, :], scalar=SLOPE, in1=z[32:33, :], op0=ALU.mult, op1=ALU.max).then_inc(s_lift, 1)
                        dve.wait_ge(s_lift, n)
                        if lag1:
                            dve.wait_ge(s_max, n - 1)
                        m = state[32:33, :, bass.ds(now, W)]
                        nc.vector.tensor_tensor(kv(drop[32:33, :]), m, kv(lift[32:33, :]), ALU.subtract).then_inc(s_drop, 1)
                        dve.wait_ge(s_drop, n)
                        nc.vector.tensor_scalar(gap[32:33, :], drop[32:33, :], 0.0, None, ALU.min)
                        nc.vector.tensor_tensor(m, m, kv(lift[32:33, :]), ALU.max).then_inc(s_max, 1)

                start_pass(nc, dve, h, r, steps, key_ready, begun, rel, True)
                turns(dve, turn)
                n = (r + 1) * NU
                base = bases(nc, mybir.EngineType.DVE, h, NU - 2, 2)
                merge_scale(n - 1, SL - 2, base[0], False)
                merge_add(n - 1, SL - 2, base[0])
                larger(n, SL - 1)
                weights(n, SL - 1)
                merge_scale(n, SL - 1, base[1], False)
                merge_add(n, SL - 1, base[1])
                dve.wait_ge(s_acc, n)
                dve.wait_ge(s_den, n)


def finish_attention(nc, h, a, acc, state, table, ypre):
    with ExitStack() as ctx:
        sb = lambda name, shape, dt=fp32: ctx.enter_context(nc.sbuf_tensor("fa_" + name, shape, dt))
        pb = lambda name: ctx.enter_context(nc.psum_tensor("fa_" + name, [P, 1024], fp32))
        sem = lambda name: ctx.enter_context(nc.semaphore("fa_" + name))
        w, bias, dw, db = sb("w", [P, NT, D]), sb("bias", [NT, D]), sb("dw", [P, D]), sb("db", [1, D])
        att = sb("att_sum", [P, NT, GN])
        x, xc = sb("x", [P, G, D]), sb("xc", [P, G, D])
        nrm = sb("nrm", [P, G, D])
        mean, var, dev, inv, eps = sb("mean", [P, G]), sb("var", [P, G]), sb("dev", [P, G]), sb("inv", [P, G]), sb("eps", [P, 1])
        ht = sb("ht", [P, GN])
        hd = sb("hd", [P, G, D])
        ps_n, ps_o, ps_h, ps_m = pb("ps_n"), pb("ps_o"), pb("ps_h"), pb("ps_m")
        (w_in, x_in, y_done, t_done, y_free, t_free, epsilon, s_den, s_rden, s_att, s_out, s_x1, s_sum, s_mean, s_cen,
         s_sq, s_var, s_dev, s_inv, s_nrm, s_relu, s_y, s_turned, s_ht, s_hd, s_hdc) = (sem("f_" + k) for k in (
             "w_in x_in y_done t_done y_free t_free eps den rden att out x1 sum mean cen sq var dev inv nrm relu y turned ht hd hdc").split())
        block = ctx.enter_context(nc.Block())

        @block.sync
        def _(sp):
            sp.sem_inc(y_free, 1)
            sp.dma_start(w[:, :, :], a["L0_gnn_W"].rearrange("t i o -> i t o")).then_inc(w_in, 16)
            sp.dma_start(bias[:, :], a["L0_gnn_bias"][:, :]).then_inc(w_in, 16)
            sp.dma_start(dw[:, :], a["L1_gnn_dW"][:, :]).then_inc(w_in, 16)
            sp.dma_start(db[:, :], a["L1_gnn_db"].rearrange("(o f) -> o f", o=1)).then_inc(w_in, 16)
            with sp.Fori(0, GROUPS) as g:
                sp.wait_ge(y_free, g + 1)
                sp.dma_start(x[:, :, :], a["x"][bass.ds(g, 1), :, :, :].rearrange("o p t f -> (o p) t f")).then_inc(x_in, 16)
                sp.wait_ge(s_y, g + 1)
                sp.dma_start(ypre[bass.ds(g, 1), :, :, :].rearrange("o p t f -> (o p) t f"), x[:, :, :]).then_inc(y_done, 16)
                sp.wait_ge(y_done, 16 * g + 16)
                sp.sem_inc(y_free, 1)

        @block.gpsimd
        def _(pool):
            pool.sem_inc(t_free, 1)
            with pool.Fori(0, GROUPS) as g:
                pool.wait_ge(s_hdc, g + 1)
                pool.dma_start(table[bass.ds(g * GN, GN), :].rearrange("(t p) r -> p t r", p=P), hd[:, :, :]).then_inc(t_done, 16)
                pool.wait_ge(t_done, 16 * g + 16)
                pool.sem_inc(t_free, 1)

        @block.tensor
        def _(pe):
            pe.wait_ge(w_in, 64)
            with pe.Fori(0, GROUPS) as g:
                for t in range(NT):
                    pe.wait_ge(s_rden, NT * g + t + 1)
                    for k in range(2):
                        last = nc.tensor.matmul(ps_n[:, k * 512:k * 512 + GN // 2], h.sel_den, state[:, t, bass.ds(g * GN + k * (GN // 2), GN // 2)],
                                                start=True, stop=True)
                    last.then_inc(s_den, 1)
                pe.wait_ge(s_att, NT * g + NT)
                for j in range(G):
                    for t in range(NT):
                        nc.tensor.matmul(ps_o[:, j * P:(j + 1) * P], att[:, t, j * P:(j + 1) * P], w[:, t, :], start=(t == 0), stop=False)
                    last = nc.tensor.matmul(ps_o[:, j * P:(j + 1) * P], h.ones[0:NT, :], bias[:, :], start=False, stop=True)
                last.then_inc(s_out, 1)
                pe.wait_ge(s_relu, g + 1)
                for j in range(G):
                    last = nc.tensor.transpose(ps_h[:, j * P:(j + 1) * P], nrm[:, j, :], h.ident)
                last.then_inc(s_turned, 1)
                pe.wait_ge(s_ht, g + 1)
                for j in range(G):
                    nc.tensor.matmul(ps_m[:, j * P:(j + 1) * P], ht[:, j * P:(j + 1) * P], dw[:, :], start=True, stop=False)
                    last = nc.tensor.matmul(ps_m[:, j * P:(j + 1) * P], h.ones[0:1, :], db[:, :], start=False, stop=True)
                last.then_inc(s_hd, 1)

        @block.scalar
        def _(act):
            act.wait_ge(epsilon, 1)
            with act.Fori(0, GROUPS) as g:
                act.wait_ge(s_var, g + 1)
                nc.scalar.activation(dev[:, :], var[:, :], ACT.Sqrt, bias=eps[:, :], scale=1.0 / D).then_inc(s_dev, 1)
                act.wait_ge(s_turned, g + 1)
                nc.scalar.copy(ht[:, :], ps_h[:, 0:GN]).then_inc(s_ht, 1)
                act.wait_ge(s_hd, g + 1)
                act.wait_ge(t_free, g + 1)
                nc.scalar.copy(hd[:, :, :].rearrange("p t f -> p (t f)"), ps_m[:, 0:GN]).then_inc(s_hdc, 1)

        @block.vector
        def _(dve):
            dve.sem_inc(s_rden, 1)
            nc.vector.memset(eps[:, :], EPS).then_inc(epsilon, 1)
            with dve.Fori(0, GROUPS) as g:
                for t in range(NT):
                    dve.wait_ge(s_den, NT * g + t + 1)
                    nc.vector.reciprocal(att[:, t, :].rearrange("p (k n) -> p k n", k=2),
                                         ps_n[:, :].rearrange("p (k n) -> p k n", k=2)[:, :, 0:GN // 2]).then_inc(s_rden, 1)
                    dve.wait_ge(s_rden, NT * g + t + 2)
                    nc.vector.tensor_tensor(att[:, t, :], acc[:, t, bass.ds(g * GN, GN)], att[:, t, :], ALU.mult).then_inc(s_att, 1)
                dve.wait_ge(x_in, 16 * g + 16)
                dve.wait_ge(s_out, g + 1)
                xf = x[:, :, :].rearrange("p t f -> p (t f)")
                nc.vector.tensor_tensor(xf, xf, ps_o[:, 0:GN], ALU.add).then_inc(s_x1, 1)
                dve.wait_ge(s_x1, g + 1)
                nc.vector.tensor_reduce(out=mean[:, :], in_=x[:, :, :], op=ALU.add, axis=AX.X).then_inc(s_sum, 1)
                dve.wait_ge(s_sum, g + 1)
                nc.vector.tensor_scalar(mean[:, :], mean[:, :], 1.0 / D, None, ALU.mult).then_inc(s_mean, 1)
                dve.wait_ge(s_mean, g + 1)
                nc.vector.tensor_tensor(xc[:, :, :], x[:, :, :], mean[:, :].unsqueeze(2).to_broadcast([P, G, D]), ALU.subtract).then_inc(s_cen, 1)
                dve.wait_ge(s_cen, g + 1)
                nc.vector.tensor_tensor(nrm[:, :, :], xc[:, :, :], xc[:, :, :], ALU.mult).then_inc(s_sq, 1)
                dve.wait_ge(s_sq, g + 1)
                nc.vector.tensor_reduce(out=var[:, :], in_=nrm[:, :, :], op=ALU.add, axis=AX.X).then_inc(s_var, 1)
                dve.wait_ge(s_dev, g + 1)
                nc.vector.reciprocal(inv[:, :], dev[:, :]).then_inc(s_inv, 1)
                dve.wait_ge(s_inv, g + 1)
                nc.vector.tensor_tensor(xc[:, :, :], xc[:, :, :], inv[:, :].unsqueeze(2).to_broadcast([P, G, D]), ALU.mult).then_inc(s_nrm, 1)
                dve.wait_ge(s_nrm, g + 1)
                nc.vector.tensor_scalar(nrm[:, :, :], xc[:, :, :], 0.0, None, ALU.max).then_inc(s_relu, 1)
                dve.wait_ge(s_relu, g + 1)
                nc.vector.tensor_tensor(x[:, :, :], x[:, :, :], nrm[:, :, :], ALU.add).then_inc(s_y, 1)


def convolution_edges(nc, h, a, acc, table):
    with ExitStack() as ctx:
        sb = lambda name, shape, dt=fp32: ctx.enter_context(nc.sbuf_tensor("ce_" + name, shape, dt))
        pb = lambda name, n=1024: ctx.enter_context(nc.psum_tensor("ce_" + name, [P, n], fp32))
        sem = lambda name: ctx.enter_context(nc.semaphore("ce_" + name))
        H = UE // 2
        fw1, fb1, fw2, fb2 = sb("fw1", [RBF, D]), sb("fb1", [D, 1]), sb("fw2", [D, D]), sb("fb2", [P, D])
        idx = [sb(f"idx{s}", [P, CH], i32) for s in range(SL)]
        xg = sb("xg", [P, XS, CH, D])
        ea = sb("ea", [RBF, XS, UE])
        hid = sb("hid", [P, 2, UE])
        flt, msg = sb("flt", [P, CH, D]), sb("msg", [P, 2, CH, D])
        hot = sb("hot", [P, 2, CH, W])
        rel = sb("rel", [P, NU, CH])
        ps_h = pb("ps_h")
        ps_f = [pb(f"ps_f{b}") for b in range(2)]
        ps_a = [pb(f"ps_a{b}", 512) for b in range(2)]
        idx_in = [sem(f"idx_in{s}") for s in range(SL)]
        sem_landed = sem("landed")
        gathered = [sem(f"gathered{s}") for s in range(XS)]
        ea_in = [sem(f"ea_in{s}") for s in range(XS)]
        (w_in, xg_free, pool_turn, ea_free, steps, key_ready, begun, cleared, s_hid, s_act, s_flt, s_bias, s_hot, s_msg, s_sum, s_acc) = (
            sem("c_" + k) for k in "w_in xg_free pool_turn ea_free steps key_ready begun cleared hid act flt bias hot msg sum acc".split())
        block = ctx.enter_context(nc.Block())

        @block.sync
        def _(sp):
            sp.dma_start(fw1[:, :], a["L1_gnn_fW1"][:, :]).then_inc(w_in, 16)
            sp.dma_start(fb1[:, :], a["L1_gnn_fb1"].rearrange("(f o) -> f o", o=1)).then_inc(w_in, 16)
            sp.dma_start(fw2[:, :], a["L1_gnn_fW2"][:, :]).then_inc(w_in, 16)
            sp.dma_start(fb2[:, :], a["L1_gnn_fb2"].rearrange("(o f) -> o f", o=1).to_broadcast([P, D])).then_inc(w_in, 16)

            def attributes(r, i, s):
                n = (r * TURNS + i) * SL + s + 1
                sp.wait_ge(s_hid, n)
                sp.dma_start(ea[:, s % XS, :], a["edge_attr_50"][:, bass.ds((i * SL + s) * UE, UE)]).then_inc(ea_in[s % XS], 16)
            load_indices(sp, a, h, idx, idx_in, gathered, sem_landed, attributes)

        @block.scalar
        def _(act):
            act.wait_ge(w_in, 64)
            with act.Fori(0, pass_count(act, h)) as r:
                def turn(i, first):
                    for s in range(SL):
                        n, b = (r * TURNS + i) * SL + s + 1, s % 2
                        act.wait_ge(s_hid, n + XS)
                        if not (first and s < 2):
                            act.wait_ge(s_flt, n - 2)
                        nc.scalar.activation(hid[:, b, :].rearrange("p (k e) -> p k e", k=2), ps_h[:, :].rearrange("p (k e) -> p k e", k=2)[:, :, 0:H],
                                             ACT.Silu, bias=fb1[:, :]).then_inc(s_act, 1)
                turns(act, turn)

        @block.gpsimd
        def _(pool):
            gather_units(pool, h, table, xg, D, idx, idx_in, gathered, s_msg, pool_turn)

        @block.tensor
        def _(pe):
            pe.sem_inc(s_hid, XS)
            pe.wait_ge(w_in, 64)
            with pe.Fori(0, pass_count(pe, h)) as r:
                def filters(n, s):
                    b = s % 2
                    pe.wait_ge(s_act, n)
                    for c in range(CH):
                        last = nc.tensor.matmul(ps_f[b][:, c * D:(c + 1) * D], hid[:, b, c * P:(c + 1) * P], fw2[:, :], start=True, stop=True)
                    last.then_inc(s_flt, 1)

                def sums(n, s):
                    b = s % 2
                    pe.wait_ge(s_msg, n + XS)
                    for c in range(CH):
                        last = nc.tensor.matmul(ps_a[b][:, 0:W], msg[:, b, c, :], hot[:, b, c, :], start=(c == 0), stop=(c == CH - 1))
                    last.then_inc(s_sum, 1)

                def turn(i, first):
                    for s in range(SL):
                        n = (r * TURNS + i) * SL + s + 1
                        if not (first and s < 1):
                            pe.wait_ge(s_act, n - 1)
                        pe.wait_ge(ea_in[s % XS], 16 * (PER * (r * TURNS + i) + s // XS + 1))
                        for k in range(2):
                            last = nc.tensor.matmul(ps_h[:, k * 512:k * 512 + H], fw1[:, :], ea[:, s % XS, k * H:(k + 1) * H], start=True, stop=True)
                        last.then_inc(s_hid, 1)
                        if not (first and s < 2):
                            sums(n - 2, s)
                        if not (first and s < 1):
                            filters(n - 1, s - 1)
                turns(pe, turn)
                n = (r + 1) * NU
                sums(n - 1, SL - 2)
                filters(n, SL - 1)
                sums(n, SL - 1)

        @block.vector
        def _(dve):
            dve.sem_inc(s_msg, XS)
            nc.vector.memset(h.sweep[:, :], 0.0).then_inc(cleared, 1)
            nc.vector.memset(acc[:, :], 0.0).then_inc(cleared, 1)
            dve.wait_ge(cleared, 2)
            dve.wait_ge(w_in, 64)
            with dve.Fori(0, pass_count(dve, h)) as r:
                def one_hot(unit, s):
                    b = s % 2
                    keys = h.key[:, bass.ds(unit, 1), :].rearrange("p o c -> p (o c)")
                    nc.vector.tensor_tensor(hot[:, b, :, :], h.iota[:, 0:W].unsqueeze(1).to_broadcast([P, CH, W]),
                                            keys.unsqueeze(2).to_broadcast([P, CH, W]), ALU.is_equal).then_inc(s_hot, 1)

                def messages(n, s, count):
                    b = s % 2
                    dve.wait_ge(s_flt, n)
                    nc.vector.tensor_tensor(flt[:, :, :], ps_f[b][:, 0:CH * D].rearrange("p (c f) -> p c f", c=CH),
                                            fb2[:, :].unsqueeze(1).to_broadcast([P, CH, D]), ALU.add).then_inc(s_bias, 1)
                    dve.wait_ge(s_bias, n)
                    dve.wait_ge(gathered[s % XS], GI * count)
                    nc.vector.tensor_tensor(msg[:, b, :, :], flt[:, :, :], xg[:, s % XS, :, :], ALU.mult).then_inc(s_msg, 1)

                def merge(n, s, base, fresh):
                    dve.wait_ge(s_sum, n)
                    if not fresh:
                        dve.wait_ge(s_acc, n - 1)
                    win = bass.ds(base, W)
                    nc.vector.tensor_tensor(acc[:, win], acc[:, win], ps_a[s % 2][:, 0:W], ALU.add).then_inc(s_acc, 1)

                def turn(i, first):
                    back = 0 if first else 2
                    base = bases(nc, mybir.EngineType.DVE, h, i * SL - back, SL + back)
                    for s in range(SL):
                        t = r * TURNS + i
                        n, v = t * SL + s + 1, (s - 1) % SL
                        if not (first and s < 1):
                            one_hot(i * SL + s - 1, v)
                        if not (first and s < 2):
                            merge(n - 2, s, base[s + back - 2], first and s == 2)
                        if not (first and s < 1):
                            messages(n - 1, v, PER * t + v // XS + 1 - (PER if s == 0 else 0))

                start_pass(nc, dve, h, r, steps, key_ready, begun, rel[:, :, :], False)
                turns(dve, turn)
                n = (r + 1) * NU
                base = bases(nc, mybir.EngineType.DVE, h, NU - 2, 2)
                one_hot(NU - 1, SL - 1)
                merge(n - 1, SL - 2, base[0], False)
                messages(n, SL - 1, PER * TURNS * (r + 1))
                merge(n, SL - 1, base[1], False)
                dve.wait_ge(s_acc, n)


def finish(nc, h, a, acc, ypre, out):
    with ExitStack() as ctx:
        sb = lambda name, shape, dt=fp32: ctx.enter_context(nc.sbuf_tensor("fi_" + name, shape, dt))
        pb = lambda name: ctx.enter_context(nc.psum_tensor("fi_" + name, [P, 1024], fp32))
        sem = lambda name: ctx.enter_context(nc.semaphore("fi_" + name))
        w1, b1, w2, b2 = sb("w1", [D, D]), sb("b1", [D, 1]), sb("w2", [D, D]), sb("b2", [1, D])
        hid, y = sb("hid", [P, GN]), sb("y", [P, G, D])
        ps_u, ps_y = pb("ps_u"), pb("ps_y")
        (w_in, y_in, y_free, out_done, s_u, s_hid, s_v, s_y) = (sem("u_" + k) for k in "w_in y_in y_free out_done u hid v y".split())
        block = ctx.enter_context(nc.Block())

        @block.sync
        def _(sp):
            sp.sem_inc(y_free, 1)
            sp.dma_start(w1[:, :], a["L1_gnn_uW1"][:, :]).then_inc(w_in, 16)
            sp.dma_start(b1[:, :], a["L1_gnn_ub1"].rearrange("(f o) -> f o", o=1)).then_inc(w_in, 16)
            sp.dma_start(w2[:, :], a["L1_gnn_uW2"][:, :]).then_inc(w_in, 16)
            sp.dma_start(b2[:, :], a["L1_gnn_ub2"].rearrange("(o f) -> o f", o=1)).then_inc(w_in, 16)
            with sp.Fori(0, GROUPS) as g:
                sp.wait_ge(y_free, g + 1)
                sp.dma_start(y[:, :, :], ypre[bass.ds(g, 1), :, :, :].rearrange("o p t f -> (o p) t f")).then_inc(y_in, 16)
                sp.wait_ge(s_y, g + 1)
                sp.dma_start(out[bass.ds(g * GN, GN), :].rearrange("(t p) f -> p t f", p=P), y[:, :, :]).then_inc(out_done, 16)
                sp.wait_ge(out_done, 16 * g + 16)
                sp.sem_inc(y_free, 1)

        @block.tensor
        def _(pe):
            pe.wait_ge(w_in, 64)
            with pe.Fori(0, GROUPS) as g:
                for k in range(2):
                    last = nc.tensor.matmul(ps_u[:, k * 512:k * 512 + GN // 2], w1[:, :], acc[:, bass.ds(g * GN + k * (GN // 2), GN // 2)], start=True, stop=True)
                last.then_inc(s_u, 1)
                pe.wait_ge(s_hid, g + 1)
                for j in range(G):
                    nc.tensor.matmul(ps_y[:, j * P:(j + 1) * P], hid[:, j * P:(j + 1) * P], w2[:, :], start=True, stop=False)
                    last = nc.tensor.matmul(ps_y[:, j * P:(j + 1) * P], h.ones[0:1, :], b2[:, :], start=False, stop=True)
                last.then_inc(s_v, 1)
                pe.wait_ge(s_y, g + 1)

        @block.scalar
        def _(act):
            act.wait_ge(w_in, 64)
            with act.Fori(0, GROUPS) as g:
                act.wait_ge(s_u, g + 1)
                nc.scalar.activation(hid[:, :].rearrange("p (k n) -> p k n", k=2), ps_u[:, :].rearrange("p (k n) -> p k n", k=2)[:, :, 0:GN // 2],
                                     ACT.Silu, bias=b1[:, :]).then_inc(s_hid, 1)

        @block.vector
        def _(dve):
            with dve.Fori(0, GROUPS) as g:
                dve.wait_ge(y_in, 16 * g + 16)
                dve.wait_ge(s_v, g + 1)
                yf = y[:, :, :].rearrange("p t f -> p (t f)")
                nc.vector.tensor_tensor(yf, yf, ps_y[:, 0:GN], ALU.add).then_inc(s_y, 1)


def program(nc, a, out):
    table0 = nc.dram_tensor("table0", (NP, ROW), fp32).ap()
    table1 = nc.dram_tensor("table1", (NP, D), fp32).ap()
    ypre = nc.dram_tensor("ypre", (GROUPS, P, G, D), fp32).ap()
    with ExitStack() as ctx:
        h = Held(nc, ctx)
        prepare_edges(nc, h, a)
        with ExitStack() as att:
            acc = att.enter_context(nc.sbuf_tensor("att_acc", [P, NT, NW], fp32))
            state = att.enter_context(nc.sbuf_tensor("state", [P, NT, NW], fp32))
            prepare_nodes(nc, h, a, acc, state, table0)
            attention_edges(nc, h, a, acc, state, table0)
            finish_attention(nc, h, a, acc, state, table1, ypre)
        acc = ctx.enter_context(nc.sbuf_tensor("conv_acc", [P, NW], fp32))
        convolution_edges(nc, h, a, acc, table1)
        finish(nc, h, a, acc, ypre, out)


def kernel(**inputs):
    import concourse.bacc as bacc
    from concourse.bass_utils import run_bass_kernel_spmd

    def padded(v, n, fill):
        return np.concatenate([v, np.full((n - v.shape[0],) + v.shape[1:], fill, v.dtype)])

    def by_unit(v, fill):
        return padded(np.asarray(v), EP, fill).reshape(NU, CH, P).transpose(0, 2, 1)

    given = {k: np.asarray(v) for k, v in inputs.items()}
    arrays = {k: given[k] for k in (
        "L0_gnn_emb_table", "L0_gnn_W", "L0_gnn_bias", "L1_gnn_fW1", "L1_gnn_fb1", "L1_gnn_fW2", "L1_gnn_fb2",
        "L1_gnn_dW", "L1_gnn_db", "L1_gnn_uW1", "L1_gnn_ub1", "L1_gnn_uW2", "L1_gnn_ub2")}
    arrays["cst"] = constants()
    arrays["x"] = padded(given["x"], NP, 0).reshape(GROUPS, G, P, D).transpose(0, 2, 1, 3)
    arrays["node_type_3"] = padded(given["node_type_3"], NP, 0).reshape(1, NP)
    arrays["src"] = by_unit(given["src"], 0)
    arrays["dst"] = by_unit(given["dst"], N).transpose(1, 0, 2)
    arrays["edge_type_3"] = by_unit(given["edge_type_3"], 0).transpose(1, 0, 2)
    arrays["edge_attr_50"] = padded(given["edge_attr_50"], EP, 0).T
    arrays["w_t"] = given["L0_gnn_W"].transpose(2, 0, 1)
    arrays["att"] = np.concatenate([given["L0_gnn_att_src"], given["L0_gnn_att_dst"]]).T

    nc = bacc.Bacc("TRN2", target_bir_lowering=False, num_devices=1)
    arrays = {"in_" + k: np.ascontiguousarray(v) for k, v in arrays.items()}
    a = {k[3:]: nc.dram_tensor(k, v.shape, mybir.dt.from_np(v.dtype), kind="ExternalInput").ap() for k, v in arrays.items()}
    out = nc.dram_tensor("out_x", (NP, D), fp32, kind="ExternalOutput").ap()
    program(nc, a, out)
    r = run_bass_kernel_spmd(nc, [arrays], core_ids=[0])
    return r.results[0]["out_x"][:N]
```

```python
import numpy as np
import concourse.bass as bass
from concourse import mybir
from contextlib import ExitStack

N, D, NT, RBF = 6250, 128, 3, 50
E = 206250
P = 128
CH = 6
UE = CH * P
SL = 6
NU = -(-E // (UE * SL)) * SL
TURNS = NU // SL
EP = NU * UE
W = 32
KEYS = NT * W
G = 7
TILES = -(-N // P)
GROUPS = TILES // G
GN = G * P
NP = TILES * P
NW = NP + W
PASSES = NP // W
ROW = 132
TQ = NU // 3
SLOPE = 0.2
EPS = 1e-5
BIG = 1e30
assert TILES % G == 0 and TQ <= P and GN // 2 <= 512

fp32, bf16 = mybir.dt.float32, mybir.dt.bfloat16
i32, u16 = mybir.dt.int32, mybir.dt.uint16
ALU, ACT, AX = mybir.AluOpType, mybir.ActivationFunctionType, mybir.AxisListType


def gather(eng, out, table, idx, done):
    eng.indirect_dma_start(out=out, out_offset=None, in_=table[:, :],
                           in_offset=bass.IndirectOffsetOnAxis(ap=idx, axis=0)).then_inc(done, 16)


class Held:

    def __init__(self, nc, ctx):
        sb = lambda name, shape, dt=fp32: ctx.enter_context(nc.sbuf_tensor(name, shape, dt))
        self.cst = sb("cst", [P, 4 * P + KEYS])
        c = self.cst
        self.ident = c[:, 0:P]
        self.ones = c[:, P:2 * P]
        self.less_row32 = c[:, 2 * P:3 * P]
        self.slope = c[:, 3 * P:4 * P]
        self.iota = c[:, 4 * P:4 * P + KEYS]
        self.dst = sb("dst", [P, NU, CH], u16)
        self.key = sb("key", [P, NU, CH], bf16)
        self.ubase = sb("ubase", [P, NU])
        self.base = sb("base", [P, NU])
        self.base_i = sb("base_i", [P, NU], i32)
        self.wide = sb("wide", [P, 1])
        self.narrow = sb("narrow", [P, 1])
        self.passes = sb("passes", [P, 1], i32)
        self.sweep = sb("sweep", [P, 1])


def constants():
    c = np.zeros((P, 4 * P + KEYS), np.float32)
    c[:, 0:P] = np.eye(P)
    c[:, P:2 * P] = 1
    c[32, 2 * P:3 * P] = -1
    c[:, 3 * P:4 * P] = SLOPE
    c[:, 4 * P:] = np.arange(KEYS)
    return c


def prepare_edges(nc, h, a, typ):
    with ExitStack() as ctx:
        dst_i = ctx.enter_context(nc.sbuf_tensor("dst_i", [P, NU, CH], i32))
        typ_i = ctx.enter_context(nc.sbuf_tensor("typ_i", [P, NU, CH], i32))
        lim = ctx.enter_context(nc.sbuf_tensor("lim", [P, 2, NU], fp32))
        col = ctx.enter_context(nc.sbuf_tensor("col", [P, 2, 3], fp32))
        span = ctx.enter_context(nc.sbuf_tensor("span", [P, NU], fp32))
        top = ctx.enter_context(nc.sbuf_tensor("top", [P, 1], fp32))
        ps_t = [ctx.enter_context(nc.psum_tensor(f"ps_t{k}", [P, 512], fp32)) for k in range(2)]
        ps_b = [ctx.enter_context(nc.psum_tensor(f"ps_b{k}", [P, 512], fp32)) for k in range(2)]
        sem = lambda name: ctx.enter_context(nc.semaphore("pe_" + name))
        cst_in, dst_in, typ_in = sem("cst_in"), sem("dst_in"), sem("typ_in")
        lims, turned, cols, spread, steps = sem("lims"), sem("turned"), sem("cols"), sem("spread"), sem("steps")
        block = ctx.enter_context(nc.Block())

        @block.sync
        def _(sp):
            sp.dma_start(h.cst[:, :], a["cst"][:, :]).then_inc(cst_in, 16)
            sp.dma_start(dst_i[:, :, :], a["dst"][:, :, :]).then_inc(dst_in, 16)
            sp.dma_start(typ_i[:, :, :], a["edge_type_3"][:, :, :]).then_inc(typ_in, 16)

        @block.vector
        def _(dve):
            nc.vector.memset(h.sweep[:, :], 0.0)
            dve.wait_ge(dst_in, 16)
            nc.vector.tensor_reduce(out=lim[:, 0, :], in_=dst_i[:, :, :], op=ALU.min, axis=AX.X)
            nc.vector.tensor_reduce(out=lim[:, 1, :], in_=dst_i[:, :, :], op=ALU.max, axis=AX.X).then_inc(lims, 1)
            nc.vector.tensor_copy(h.dst[:, :, :], dst_i[:, :, :])
            dve.wait_ge(typ_in, 16)
            nc.vector.tensor_copy(typ[:, :, :], typ_i[:, :, :])
            dve.wait_ge(turned, 1)
            for k, op in enumerate((ALU.min, ALU.max)):
                nc.vector.tensor_reduce(out=col[0:TQ, k, :], in_=ps_t[k][0:TQ, 0:3 * P].rearrange("u (q p) -> u q p", q=3),
                                        op=op, axis=AX.X).then_inc(cols, 1)
            dve.wait_ge(spread, 1)
            nc.vector.tensor_copy(h.ubase[:, :], ps_b[0][:, 0:NU]).then_inc(steps, 1)
            dve.wait_ge(steps, 1)
            nc.vector.tensor_tensor(span[:, :], ps_b[1][:, 0:NU], h.ubase[:, :], ALU.subtract).then_inc(steps, 1)
            dve.wait_ge(steps, 2)
            nc.vector.tensor_reduce(out=top[:, :], in_=span[:, :], op=ALU.max, axis=AX.X).then_inc(steps, 1)
            dve.wait_ge(steps, 3)
            nc.vector.tensor_scalar(h.wide[:, :], top[:, :], W - 0.5, None, ALU.is_gt).then_inc(steps, 1)
            dve.wait_ge(steps, 4)
            nc.vector.tensor_scalar(h.narrow[:, :], h.wide[:, :], -1.0, 1.0, ALU.mult, ALU.add)
            nc.vector.tensor_scalar(h.passes[:, :], h.wide[:, :], PASSES - 1.0, 1.0, ALU.mult, ALU.add)

        @block.tensor
        def _(pe):
            pe.wait_ge(cst_in, 16)
            pe.wait_ge(lims, 1)
            for k in range(2):
                for q in range(3):
                    last = nc.tensor.transpose(ps_t[k][0:TQ, q * P:(q + 1) * P], lim[:, k, q * TQ:(q + 1) * TQ], h.ident)
            last.then_inc(turned, 1)
            pe.wait_ge(cols, 2)
            for k in range(2):
                for q in range(3):
                    last = nc.tensor.matmul(ps_b[k][:, q * TQ:(q + 1) * TQ],
                                            col[0:TQ, k, q:q + 1].to_broadcast([TQ, P]), h.ident[0:TQ, 0:TQ],
                                            start=True, stop=True)
            last.then_inc(spread, 1)


def prepare_nodes(nc, h, a, acc, state, table):
    with ExitStack() as ctx:
        sb = lambda name, shape, dt=fp32: ctx.enter_context(nc.sbuf_tensor("pn_" + name, shape, dt))
        pb = lambda name: ctx.enter_context(nc.psum_tensor("pn_" + name, [P, 1024], fp32))
        sem = lambda name: ctx.enter_context(nc.semaphore("pn_" + name))
        wt, att, emb = sb("wt", [P, NT, D]), sb("att", [P, 2 * NT]), sb("emb", [3, D])
        score = sb("score", [P, 2 * NT])
        rows_w = sb("rows_w", [P, NT, 96])
        nt_i, nt1h = sb("nt_i", [3, GN], i32), sb("nt1h", [3, GN])
        kind = sb("kind", [P, 1])
        kind_i = sb("kind_i", [P, 1], i32)
        x, xc, sq = sb("x", [P, G, D]), sb("xc", [P, G, D]), sb("sq", [P, G, D])
        mean, var = sb("mean", [P, G]), sb("var", [P, G])
        dev, inv = sb("dev", [P, G]), sb("inv", [P, G])
        rows = sb("rows", [P, G, ROW])
        xt = sb("xt", [P, GN])
        ps_e, ps_x, ps_r = pb("ps_e"), pb("ps_x"), pb("ps_r")
        ps_s = ctx.enter_context(nc.psum_tensor("ps_s", [P, 512], fp32))
        w_in, att_in, emb_in, x_in, nt_in, out_done = sem("w_in"), sem("att_in"), sem("emb_in"), sem("x_in"), sem("nt_in"), sem("out_done")
        sc_ps, sc_ok, x_used, nt_used, onehot, emb_ok = sem("sc_ps"), sem("sc_ok"), sem("x_used"), sem("nt_used"), sem("onehot"), sem("emb_ok")
        n_sum, n_mean, n_cen, n_sq, n_var, n_dev, n_inv = (sem(f"n_{k}") for k in ("sum", "mean", "cen", "sq", "var", "dev", "inv"))
        n_nrm, feat, xt_ps, xt_ok, as_ps, as_ok = sem("n_nrm"), sem("feat"), sem("xt_ps"), sem("xt_ok"), sem("as_ps"), sem("as_ok")
        row_ps, row_out, m_ok, acc_ok, cleared, prep = sem("row_ps"), sem("row_out"), sem("m_ok"), sem("acc_ok"), sem("cleared"), sem("prep")
        eps = sb("eps", [P, 1])
        epsilon, rows_free = sem("epsilon"), sem("rows_free")
        block = ctx.enter_context(nc.Block())

        @block.sync
        def _(sp):
            sp.sem_inc(rows_free, 1)
            sp.dma_start(wt[:, :, :], a["w_t"][:, :, :]).then_inc(w_in, 16)
            sp.dma_start(att[:, :], a["att"][:, :]).then_inc(att_in, 16)
            sp.dma_start(emb[:, :], a["L0_gnn_emb_table"][:, :]).then_inc(emb_in, 16)
            sp.dma_start(x[:, :, :], a["x"][0, :, :, :]).then_inc(x_in, 16)
            sp.dma_start(nt_i[:, :], a["node_type_3"][0:1, 0:GN].to_broadcast([3, GN])).then_inc(nt_in, 16)
            with sp.Fori(0, GROUPS - 1) as g:
                sp.wait_ge(x_used, g + 1)
                sp.dma_start(x[:, :, :], a["x"][bass.ds(g + 1, 1), :, :, :].rearrange("o p t f -> (o p) t f")).then_inc(x_in, 16)
                sp.wait_ge(onehot, g + 1)
                sp.dma_start(nt_i[:, :], a["node_type_3"][0:1, bass.ds((g + 1) * GN, GN)].to_broadcast([3, GN])).then_inc(nt_in, 16)
                sp.wait_ge(feat, g + 1)
                sp.wait_ge(as_ok, g + 1)
                sp.dma_start(table[bass.ds(g * GN, GN), :].rearrange("(t p) r -> p t r", p=P), rows[:, :, :]).then_inc(out_done, 16)
                sp.wait_ge(out_done, 16 * g + 16)
                sp.sem_inc(rows_free, 1)
            sp.wait_ge(feat, GROUPS)
            sp.wait_ge(as_ok, GROUPS)
            sp.dma_start(table[(GROUPS - 1) * GN:GROUPS * GN, :].rearrange("(t p) r -> p t r", p=P), rows[:, :, :]).then_inc(out_done, 16)
            sp.wait_ge(out_done, 16 * GROUPS)

        @block.gpsimd
        def _(pool):
            pool.sem_inc(acc_ok, 1)
            pool.iota(kind_i[:, :], pattern=[[0, 1]], base=0, channel_multiplier=1).then_inc(prep, 1)
            pool.wait_ge(prep, 1)
            pool.tensor_copy(kind[:, :], kind_i[:, :]).then_inc(prep, 1)
            for k, (part, value) in enumerate(((state[64:P, :, :], 1.0), (state[0:64, :, NP:NW], 0.0), (acc[:, :, NP:NW], 0.0))):
                pool.wait_ge(prep, k + 2)
                pool.memset(part, value).then_inc(prep, 1)
            pool.wait_ge(prep, 5)
            with pool.Fori(0, GROUPS) as g:
                pool.wait_ge(xt_ok, g + 1)
                for t in range(NT):
                    last = pool.tensor_copy(acc[:, t, bass.ds(g * GN, GN)], xt[:, :])
                last.then_inc(acc_ok, 1)

        @block.tensor
        def _(pe):
            pe.wait_ge(w_in, 16)
            pe.wait_ge(att_in, 16)
            for t in range(NT):
                for k in range(2):
                    c = k * NT + t
                    last = nc.tensor.matmul(ps_s[:, c:c + 1], wt[:, t, :], att[:, c:c + 1], start=True, stop=True)
            last.then_inc(sc_ps, 1)
            pe.wait_ge(emb_in, 16)
            pe.wait_ge(sc_ok, 2)
            with pe.Fori(0, GROUPS) as g:
                pe.wait_ge(onehot, g + 1)
                for t in range(G):
                    last = nc.tensor.matmul(ps_e[:, t * P:(t + 1) * P], nt1h[:, t * P:(t + 1) * P], emb[:, :], start=True, stop=True)
                last.then_inc(emb_ok, 1)
                pe.wait_ge(feat, g + 1)
                for t in range(G):
                    last = nc.tensor.transpose(ps_x[:, t * P:(t + 1) * P], rows[:, t, 0:D], h.ident)
                last.then_inc(xt_ps, 1)
                pe.wait_ge(xt_ok, g + 1)
                for t in range(G):
                    last = nc.tensor.matmul(ps_s[:, 8 + NT * t:8 + NT * t + NT], xt[:, t * P:(t + 1) * P], score[:, 0:NT], start=True, stop=True)
                last.then_inc(as_ps, 1)
                for t in range(NT):
                    pe.wait_ge(row_out, g * NT + t + 1)
                    for k in range(2):
                        last = nc.tensor.matmul(ps_r[0:96, k * 512:k * 512 + GN // 2], rows_w[:, t, :],
                                                xt[:, k * GN // 2:(k + 1) * GN // 2], start=True, stop=True)
                    last.then_inc(row_ps, 1)

        @block.scalar
        def _(act):
            act.wait_ge(epsilon, 1)
            act.sem_inc(row_out, 1)
            with act.Fori(0, GROUPS) as g:
                act.wait_ge(n_var, g + 1)
                nc.scalar.activation(dev[:, :], var[:, :], ACT.Sqrt, bias=eps[:, :], scale=1.0 / D).then_inc(n_dev, 1)
                for t in range(NT):
                    act.wait_ge(row_ps, g * NT + t + 1)
                    nc.scalar.copy(state[0:64, t, bass.ds(g * GN, GN)].rearrange("p (k n) -> p k n", k=2),
                                   ps_r[0:64, :].rearrange("p (k n) -> p k n", k=2)[:, :, 0:GN // 2]).then_inc(row_out, 1)

        @block.vector
        def _(dve):
            nc.vector.memset(eps[:, :], EPS).then_inc(epsilon, 1)
            nc.vector.memset(rows[:, :, D + NT:ROW], 0.0)
            nc.vector.memset(rows_w[:, :, :], 0.0).then_inc(sc_ok, 1)
            dve.wait_ge(sc_ps, 1)
            nc.vector.tensor_copy(score[:, :], ps_s[:, 0:2 * NT]).then_inc(n_cen, 1)
            dve.wait_ge(n_cen, 1)
            dve.wait_ge(sc_ok, 1)
            nc.vector.tensor_copy(rows_w[:, :, 0], score[:, NT:2 * NT])
            nc.vector.tensor_tensor(rows_w[:, :, 32], score[:, 0:NT], score[:, NT:2 * NT], ALU.add).then_inc(sc_ok, 1)
            dve.wait_ge(prep, 2)
            with dve.Fori(0, GROUPS) as g:
                dve.wait_ge(nt_in, 16 * g + 16)
                nc.vector.tensor_scalar(nt1h[:, :], nt_i[:, :], kind[0:3, :], None, ALU.is_equal).then_inc(onehot, 1)
                dve.wait_ge(x_in, 16 * g + 16)
                nc.vector.tensor_reduce(out=mean[:, :], in_=x[:, :, :], op=ALU.add, axis=AX.X).then_inc(n_sum, 1)
                dve.wait_ge(n_sum, g + 1)
                nc.vector.tensor_scalar(mean[:, :], mean[:, :], 1.0 / D, None, ALU.mult).then_inc(n_mean, 1)
                dve.wait_ge(n_mean, g + 1)
                nc.vector.tensor_tensor(xc[:, :, :], x[:, :, :], mean[:, :].unsqueeze(2).to_broadcast([P, G, D]), ALU.subtract).then_inc(x_used, 1)
                dve.wait_ge(x_used, g + 1)
                nc.vector.tensor_tensor(sq[:, :, :], xc[:, :, :], xc[:, :, :], ALU.mult).then_inc(n_sq, 1)
                dve.wait_ge(n_sq, g + 1)
                nc.vector.tensor_reduce(out=var[:, :], in_=sq[:, :, :], op=ALU.add, axis=AX.X).then_inc(n_var, 1)
                dve.wait_ge(n_dev, g + 1)
                nc.vector.reciprocal(inv[:, :], dev[:, :]).then_inc(n_inv, 1)
                dve.wait_ge(n_inv, g + 1)
                nc.vector.tensor_tensor(xc[:, :, :], xc[:, :, :], inv[:, :].unsqueeze(2).to_broadcast([P, G, D]), ALU.mult).then_inc(n_nrm, 1)
                dve.wait_ge(n_nrm, g + 1)
                dve.wait_ge(emb_ok, g + 1)
                dve.wait_ge(rows_free, g + 1)
                nc.vector.scalar_tensor_tensor(out=rows[:, :, 0:D], in0=xc[:, :, :], scalar=0.0,
                                               in1=ps_e[:, 0:GN].rearrange("p (t f) -> p t f", t=G),
                                               op0=ALU.max, op1=ALU.add).then_inc(feat, 1)
                dve.wait_ge(xt_ps, g + 1)
                dve.wait_ge(acc_ok, g + 1)
                nc.vector.tensor_copy(xt[:, :], ps_x[:, 0:GN]).then_inc(xt_ok, 1)
                dve.wait_ge(as_ps, g + 1)
                nc.vector.tensor_copy(rows[:, :, D:D + NT], ps_s[:, 8:8 + NT * G].rearrange("p (t k) -> p t k", k=NT)).then_inc(as_ok, 1)
                dve.wait_ge(row_out, NT * g + NT + 1)
                nc.vector.scalar_tensor_tensor(out=state[32:64, :, bass.ds(g * GN, GN)], in0=state[32:64, :, bass.ds(g * GN, GN)],
                                               scalar=SLOPE, in1=state[32:64, :, bass.ds(g * GN, GN)],
                                               op0=ALU.mult, op1=ALU.max).then_inc(m_ok, 1)


STEPS = 8


def start_pass(nc, dve, h, r, steps, key_ready, begun, rel, typ=None):
    done = [0]

    def link(ins):
        done[0] += 1
        ins.then_inc(steps, 1)
        dve.wait_ge(steps, r * STEPS + done[0])

    link(nc.vector.tensor_tensor(h.base[:, :], h.ubase[:, :], h.narrow[:, :].to_broadcast([P, NU]), ALU.mult))
    link(nc.vector.tensor_tensor(h.base[:, :], h.base[:, :], h.sweep[:, :].to_broadcast([P, NU]), ALU.add))
    nc.vector.tensor_copy(h.base_i[:, :], h.base[:, :])
    link(nc.vector.tensor_tensor(rel, h.dst[:, :, :], h.base[:, :].unsqueeze(2).to_broadcast([P, NU, CH]), ALU.subtract))
    link(nc.vector.scalar_tensor_tensor(out=h.sweep[:, :], in0=h.wide[:, :], scalar=float(W), in1=h.sweep[:, :], op0=ALU.mult, op1=ALU.add))
    link(nc.vector.tensor_scalar(h.key[:, :, :], rel, -0.5, None, ALU.is_gt))
    link(nc.vector.scalar_tensor_tensor(out=h.key[:, :, :], in0=rel, scalar=W - 0.5, in1=h.key[:, :, :], op0=ALU.is_lt, op1=ALU.mult))
    if typ is not None:
        link(nc.vector.scalar_tensor_tensor(out=rel, in0=typ[:, :, :], scalar=float(W), in1=rel, op0=ALU.mult, op1=ALU.add))
    link(nc.vector.scalar_tensor_tensor(out=rel, in0=rel, scalar=1.0, in1=h.key[:, :, :], op0=ALU.add, op1=ALU.mult))
    if typ is None:
        done[0] += 1
        dve.sem_inc(steps, 1)
    assert done[0] == STEPS
    nc.vector.tensor_scalar(h.key[:, :, :], rel, -1.0, None, ALU.add).then_inc(key_ready, 1)
    dve.wait_ge(key_ready, r + 1)
    dve.sem_inc(begun, 1)


def pass_count(eng, h):
    return eng.value_load(h.passes[0:1, 0:1], min_val=1, max_val=PASSES)


def bases(nc, engine, h, first, count):
    return nc.values_load_multi_w_load_instructions(h.base_i[0:1, bass.ds(first, count)], engines=[engine],
                                                    min_val=0, max_val=N)[1]


def turns(eng, body):
    body(0, True)
    with eng.Fori(1, TURNS) as i:
        body(i, False)


def load_indices(sp, a, h, idx, idx_in, gathered, landed, also=lambda r, i, s: None):
    for s in range(SL):
        sp.dma_start(idx[s][:, :], a["src"][s, :, :]).then_inc(idx_in[s], 16)
    passes = pass_count(sp, h)
    with sp.Fori(0, passes) as r:
        with sp.Fori(0, TURNS - 1) as i:
            for s in range(SL):
                also(r, i, s)
                sp.wait_ge(gathered[s % XS], GI * (PER * (r * TURNS + i) + s // XS + 1))
                sp.dma_start(idx[s][:, :], a["src"][bass.ds((i + 1) * SL + s, 1), :, :].rearrange("o p c -> (o p) c")).then_inc(idx_in[s], 16)
        for s in range(SL):
            also(r, TURNS - 1, s)
            sp.wait_ge(gathered[s % XS], GI * (PER * (r * TURNS + TURNS - 1) + s // XS + 1))
            sp.dma_start(idx[s][:, :], a["src"][s, :, :]).then_inc(idx_in[s], 16)
    for s in range(SL):
        sp.wait_ge(idx_in[s], 16 * (passes * TURNS + 1))
    sp.sem_inc(landed, 1)


def gather_units(pool, h, table, xg, width, idx, idx_in, gathered, xg_free, pool_turn):
    with pool.Fori(0, pass_count(pool, h)) as r:
        with pool.Fori(0, TURNS) as i:
            for s in range(SL):
                pool.wait_ge(idx_in[s], 16 * (r * TURNS + i + 1))
                pool.wait_ge(xg_free, (r * TURNS + i) * SL + s + 1)
                pool.sem_inc(pool_turn, 1)
                for c in range(CH):
                    gather(pool, xg[:, s % XS, c, 0:width], table, idx[s][:, c:c + 1], gathered[s % XS])


XS = 6
PER = SL // XS
GI = 16 * CH


def attention_edges(nc, h, a, acc, state, typ, table):
    with ExitStack() as ctx:
        sb = lambda name, shape, dt=fp32: ctx.enter_context(nc.sbuf_tensor("ae_" + name, shape, dt))
        pb = lambda name: ctx.enter_context(nc.psum_tensor("ae_" + name, [P, 512], fp32))
        sem = lambda name: ctx.enter_context(nc.semaphore("ae_" + name))
        idx = [sb(f"idx{s}", [P, CH], i32) for s in range(SL)]
        xg = sb("xg", [P, XS, CH, ROW])
        oh3, pick = sb("oh3", [P, CH, NT], bf16), sb("pick", [P, CH, NT])
        sc, sc2 = sb("sc", [P, 2, CH]), sb("sc2", [P, 2, CH])
        off = sb("off", [P, 3, CH, KEYS], bf16)
        e = sb("e", [P, 3, CH * KEYS])
        masked = e[:, 2, :].rearrange("p (c k) -> p c k", c=CH)
        by_chunk = [e[:, b, :].rearrange("p (c k) -> p c k", c=CH) for b in range(2)]
        rel = e[:, :, :].rearrange("p a k -> p (a k)")[:, 0:NU * CH].rearrange("p (u c) -> p u c", c=CH)
        high, high_k = sb("high", [P, KEYS]), sb("high_k", [KEYS, 1])
        top, rise = sb("top", [64, KEYS]), sb("rise", [64, 2, KEYS])
        rescale = sb("rescale", [P, 2, KEYS])
        ps_t, ps_z = pb("ps_t"), pb("ps_z")
        ps_c, ps_a, ps_d = ([pb(f"ps_{k}{b}") for b in range(2)] for k in "cad")
        idx_in = [sem(f"idx_in{s}") for s in range(SL)]
        gathered = [sem(f"gathered{s}") for s in range(XS)]
        landed, xg_free, pool_turn, steps, key_ready, begun, rise_zero = (
            sem(k) for k in "landed xg_free pool_turn steps key_ready begun rise_zero".split())
        (s_oh, s_pick, s_score, s_off, s_masked, s_high, s_turned, s_highk, s_z, s_top, s_new, s_rise, s_max,
         s_dst, s_c, s_pre, s_sub, s_e, s_wgt, s_sum, s_scaled, s_dscaled, s_acc, s_den) = (sem("s_" + k) for k in (
             "oh pick score off masked high turned highk z top new rise max dst c pre sub e wgt sum scaled dscaled acc den").split())
        block = ctx.enter_context(nc.Block())

        def kv(ap):
            return ap.rearrange("p (t n) -> p t n", t=NT)

        @block.sync
        def _(sp):
            load_indices(sp, a, h, idx, idx_in, gathered, landed)

        @block.gpsimd
        def _(pool):
            gather_units(pool, h, table, xg, ROW, idx, idx_in, gathered, xg_free, pool_turn)

        @block.scalar
        def _(act):
            with act.Fori(0, pass_count(act, h)) as r:
                def exps(n, s):
                    b = s % 2
                    act.wait_ge(s_sub, n)
                    for c in range(CH):
                        nc.scalar.activation(by_chunk[b][:, c, :], by_chunk[b][:, c, :], ACT.Exp, bias=sc2[:, b, c:c + 1])
                    nc.scalar.activation(rescale[:, b, :], ps_c[b][:, 2 * KEYS:3 * KEYS], ACT.Exp).then_inc(s_e, 1)

                def turn(i, first):
                    for s in range(SL):
                        n, b = (r * TURNS + i) * SL + s + 1, s % 2
                        if not (first and s < 1):
                            exps(n - 1, (s - 1) % SL)
                        if not (first and s < 2):
                            act.wait_ge(s_sum, n - 2)
                        act.wait_ge(s_dst, n)
                        act.wait_ge(s_score, n)
                        for c in range(CH):
                            last = nc.scalar.activation(by_chunk[b][:, c, :], ps_c[b][:, 0:KEYS], ACT.Relu, bias=sc[:, b, c:c + 1])
                        last.then_inc(s_pre, 1)
                turns(act, turn)
                exps((r + 1) * NU, SL - 1)

        @block.tensor
        def _(pe):
            pe.sem_inc(xg_free, XS)
            pe.wait_ge(rise_zero, 1)
            with pe.Fori(0, pass_count(pe, h)) as r:
                def sums(n, s, chunks):
                    b = s % 2
                    for c in chunks:
                        last = nc.tensor.matmul(ps_a[b][:, 0:KEYS], xg[:, s % XS, c, 0:D], by_chunk[b][:, c, :], start=(c == 0), stop=(c == CH - 1))
                    if CH - 1 in chunks:
                        last.then_inc(xg_free, 1)
                        for c in range(CH):
                            last = nc.tensor.matmul(ps_d[b][64:65, 0:KEYS], h.ones[:, 0:1], by_chunk[b][:, c, :], start=(c == 0), stop=(c == CH - 1))
                        last.then_inc(s_sum, 1)

                def turn(i, first):
                    base = bases(nc, mybir.EngineType.PE, h, i * SL, SL)
                    for s in range(SL):
                        n, b = (r * TURNS + i) * SL + s + 1, s % 2
                        lag1 = not (first and s < 1)
                        nc.tensor.matmul(kv(ps_c[b][:, 0:KEYS]), h.ones[0:1, :], state[0:1, :, bass.ds(base[s], W)], start=True, stop=True)
                        nc.tensor.matmul(kv(ps_c[b][:, KEYS:2 * KEYS]), h.slope[0:1, :], state[0:1, :, bass.ds(base[s], W)], start=True, stop=False).then_inc(s_dst, 1)
                        pe.wait_ge(s_high, n)
                        nc.tensor.transpose(ps_t[0:KEYS, 0:P], high[:, :], h.ident).then_inc(s_turned, 1)
                        pe.wait_ge(s_highk, n)
                        nc.tensor.matmul(ps_z[0:65, 0:KEYS], high_k[:, :].to_broadcast([KEYS, 65]), h.ident[0:KEYS, 0:KEYS], start=True, stop=False)
                        nc.tensor.matmul(kv(ps_z[0:65, 0:KEYS]), h.ones[0:1, 0:65], state[0:1, :, bass.ds(base[s], W)], start=False, stop=True).then_inc(s_z, 1)
                        if lag1:
                            pe.wait_ge(s_wgt, n - 1)
                            sums(n - 1, (s - 1) % SL, range(0, CH // 2))
                        pe.wait_ge(s_pre, n)
                        pe.wait_ge(s_rise, n)
                        nc.tensor.matmul(ps_c[b][:, KEYS:2 * KEYS], h.less_row32[0:64, :], rise[:, 0, :], start=False, stop=True)
                        nc.tensor.matmul(ps_c[b][:, 2 * KEYS:3 * KEYS], h.less_row32[0:64, :], rise[:, 1, :], start=True, stop=True).then_inc(s_c, 1)
                        if lag1:
                            sums(n - 1, (s - 1) % SL, range(CH // 2, CH))
                pe.wait_ge(key_ready, r + 1)
                pe.sem_inc(begun, 1)
                turns(pe, turn)
                pe.wait_ge(s_wgt, (r + 1) * NU)
                sums((r + 1) * NU, SL - 1, range(CH))

        @block.vector
        def _(dve):
            nc.vector.memset(rise[:, :, :], 0.0).then_inc(rise_zero, 1)
            with dve.Fori(0, pass_count(dve, h)) as r:
                def look_up(n, s, i, unit, part):
                    b = s % 2
                    if part == "off":
                        keys = h.key[:, bass.ds(unit, 1), :].rearrange("p o c -> p (o c)")
                        nc.vector.tensor_tensor(off[:, s % 3, :, :], h.iota.unsqueeze(1).to_broadcast([P, CH, KEYS]),
                                                keys.unsqueeze(2).to_broadcast([P, CH, KEYS]), ALU.not_equal).then_inc(s_off, 1)
                    elif part == "pick":
                        types = typ[:, bass.ds(unit, 1), :].rearrange("p o c -> p (o c)")
                        nc.vector.tensor_tensor(oh3[:, :, :], types.unsqueeze(2).to_broadcast([P, CH, NT]),
                                                h.iota[:, 0:NT].unsqueeze(1).to_broadcast([P, CH, NT]), ALU.is_equal).then_inc(s_oh, 1)
                        dve.wait_ge(gathered[s % XS], GI * (PER * (r * TURNS + i) + s // XS + 1))
                        dve.wait_ge(s_oh, n)
                        nc.vector.tensor_tensor(pick[:, :, :], oh3[:, :, :], xg[:, s % XS, :, D:D + NT], ALU.mult).then_inc(s_pick, 1)
                    elif part == "score":
                        dve.wait_ge(s_pick, n)
                        nc.vector.tensor_reduce(out=sc[:, b, :], in_=pick[:, :, :], op=ALU.add, axis=AX.X).then_inc(s_score, 1)
                    else:
                        dve.wait_ge(s_score, n)
                        nc.vector.tensor_scalar(sc2[:, b, :], sc[:, b, :], SLOPE, None, ALU.mult)

                def mask(n, s):
                    dve.wait_ge(s_off, n)
                    dve.wait_ge(s_score, n)
                    nc.vector.scalar_tensor_tensor(out=masked, in0=off[:, s % 3, :, :], scalar=-BIG,
                                                   in1=sc[:, s % 2, :].unsqueeze(2).to_broadcast([P, CH, KEYS]), op0=ALU.mult, op1=ALU.add).then_inc(s_masked, 1)

                def highest(n):
                    dve.wait_ge(s_masked, n)
                    nc.vector.tensor_reduce(out=high[:, :], in_=masked.rearrange("p c k -> p k c"), op=ALU.max, axis=AX.X).then_inc(s_high, 1)

                def highest_key(n):
                    dve.wait_ge(s_turned, n)
                    nc.vector.tensor_reduce(out=high_k[:, :], in_=ps_t[0:KEYS, 0:P], op=ALU.max, axis=AX.X).then_inc(s_highk, 1)

                def raise_max(n, base, part, fresh):
                    m = state[32:33, :, bass.ds(base, W)]
                    if part == 0:
                        if not fresh:
                            dve.wait_ge(s_max, n - 1)
                        dve.wait_ge(s_z, n)
                        nc.vector.tensor_tensor(kv(top[32:33, :]), kv(ps_z[32:33, 0:KEYS]), m, ALU.max).then_inc(s_top, 1)
                    elif part == 1:
                        dve.wait_ge(s_top, n)
                        nc.vector.scalar_tensor_tensor(out=rise[32:33, 0, :], in0=ps_z[32:33, 0:KEYS], scalar=SLOPE, in1=top[32:33, :],
                                                       op0=ALU.mult, op1=ALU.max).then_inc(s_new, 1)
                    elif part == 2:
                        dve.wait_ge(s_new, n)
                        nc.vector.tensor_tensor(kv(rise[32:33, 1, :]), kv(rise[32:33, 0, :]), m, ALU.subtract).then_inc(s_rise, 1)
                    else:
                        dve.wait_ge(s_rise, n)
                        nc.vector.tensor_tensor(m, m, kv(rise[32:33, 0, :]), ALU.max).then_inc(s_max, 1)

                def less_max(n, s):
                    b = s % 2
                    dve.wait_ge(s_pre, n)
                    dve.wait_ge(s_c, n)
                    nc.vector.scalar_tensor_tensor(out=by_chunk[b], in0=by_chunk[b], scalar=1.0 - SLOPE,
                                                   in1=ps_c[b][:, KEYS:2 * KEYS].unsqueeze(1).to_broadcast([P, CH, KEYS]),
                                                   op0=ALU.mult, op1=ALU.add).then_inc(s_sub, 1)

                def weights(n, s):
                    b = s % 2
                    dve.wait_ge(s_e, n)
                    nc.vector.scalar_tensor_tensor(out=e[:, b, :], in0=off[:, s % 3, :, :].rearrange("p c k -> p (c k)"), scalar=0.0,
                                                   in1=e[:, b, :], op0=ALU.is_equal, op1=ALU.min).then_inc(s_wgt, 1)

                def scale_sums(n, s, base, fresh):
                    win = bass.ds(base, W)
                    if not fresh:
                        dve.wait_ge(s_acc, n - 1)
                    nc.vector.tensor_tensor(acc[:, :, win], acc[:, :, win], kv(rescale[:, s % 2, :]), ALU.mult).then_inc(s_scaled, 1)

                def scale_denominators(n, s, base, fresh):
                    win = bass.ds(base, W)
                    if not fresh:
                        dve.wait_ge(s_den, n - 1)
                    nc.vector.tensor_tensor(state[64:65, :, win], state[64:65, :, win], kv(rescale[64:65, s % 2, :]), ALU.mult).then_inc(s_dscaled, 1)

                def add_sums(n, s, base):
                    b = s % 2
                    win = bass.ds(base, W)
                    dve.wait_ge(s_scaled, n)
                    dve.wait_ge(s_sum, n)
                    nc.vector.tensor_tensor(acc[:, :, win], acc[:, :, win], kv(ps_a[b][:, 0:KEYS]), ALU.add).then_inc(s_acc, 1)
                    dve.wait_ge(s_dscaled, n)
                    nc.vector.tensor_tensor(state[64:65, :, win], state[64:65, :, win], kv(ps_d[b][64:65, 0:KEYS]), ALU.add).then_inc(s_den, 1)

                def step(n, s, i, unit, base, stages, fresh):
                    look, chain, weigh, merge = (k in stages for k in range(4))
                    if chain:
                        mask(n - 1, s - 1)
                    if weigh:
                        less_max(n - 2, s - 2)
                    if chain:
                        highest(n - 1)
                    if look:
                        look_up(n, s, i, unit, "off")
                    if chain:
                        highest_key(n - 1)
                    if weigh:
                        weights(n - 2, s - 2)
                    if merge:
                        add_sums(n - 3, s - 3, base(3))
                    if look:
                        look_up(n, s, i, unit, "pick")
                    if chain:
                        raise_max(n - 1, base(1), 0, fresh and s == 1)
                    if weigh:
                        scale_sums(n - 2, s - 2, base(2), fresh and s == 2)
                    if chain:
                        raise_max(n - 1, base(1), 1, False)
                    if look:
                        look_up(n, s, i, unit, "score")
                    if chain:
                        raise_max(n - 1, base(1), 2, False)
                    if weigh:
                        scale_denominators(n - 2, s - 2, base(2), fresh and s == 2)
                    if chain:
                        raise_max(n - 1, base(1), 3, False)
                    if look:
                        look_up(n, s, i, unit, "twice")

                def turn(i, first):
                    back = 0 if first else 3
                    base = bases(nc, mybir.EngineType.DVE, h, i * SL - back, SL - 1 + back)
                    for s in range(SL):
                        step((r * TURNS + i) * SL + s + 1, s, i, i * SL + s, lambda k: base[s + back - k],
                             [k for k in range(4) if not first or k <= s], first)

                start_pass(nc, dve, h, r, steps, key_ready, begun, rel, typ)
                turns(dve, turn)
                base = bases(nc, mybir.EngineType.DVE, h, NU - 3, 3)
                for s in range(3):
                    step((r + 1) * NU + s + 1, s, None, None, lambda k: base[s + 3 - k], range(s + 1, 4), False)
                dve.wait_ge(s_acc, (r + 1) * NU)
                dve.wait_ge(s_den, (r + 1) * NU)


def invert_denominators(nc, state, den, rden):
    part = NT * NP // P
    flat = lambda t: t.rearrange("t n -> (t n)").rearrange("(p c) -> p c", p=P)
    with nc.sbuf_tensor("id_v", [P, part], fp32) as v, nc.sbuf_tensor("id_w", [P, part], fp32) as w, \
            nc.semaphore("id_out") as den_out, nc.semaphore("id_in") as den_in, nc.semaphore("id_inv") as inverted, \
            nc.semaphore("id_done") as rden_out, nc.Block() as block:

        @block.sync
        def _(sp):
            sp.dma_start(den.rearrange("(o t) n -> o t n", o=1), state[64:65, :, 0:NP]).then_inc(den_out, 16)
            sp.wait_ge(den_out, 16)
            sp.dma_start(v[:, :], flat(den)).then_inc(den_in, 16)
            sp.wait_ge(inverted, 1)
            sp.dma_start(flat(rden), w[:, :]).then_inc(rden_out, 16)
            sp.wait_ge(rden_out, 16)

        @block.vector
        def _(dve):
            dve.wait_ge(den_in, 16)
            nc.vector.reciprocal(w[:, :], v[:, :]).then_inc(inverted, 1)


def finish_attention(nc, h, a, acc, rden, table, ypre):
    with ExitStack() as ctx:
        sb = lambda name, shape, dt=fp32: ctx.enter_context(nc.sbuf_tensor("fa_" + name, shape, dt))
        pb = lambda name: ctx.enter_context(nc.psum_tensor("fa_" + name, [P, 1024], fp32))
        sem = lambda name: ctx.enter_context(nc.semaphore("fa_" + name))
        w, bias, dw, db = sb("w", [P, NT, D]), sb("bias", [NT, D]), sb("dw", [P, D]), sb("db", [1, D])
        inv_den, att = sb("inv_den", [P, NT, GN]), sb("att_sum", [P, NT, GN])
        x, xc, sq, nrm, y = (sb(k, [P, G, D]) for k in ("x", "xc", "sq", "nrm", "y"))
        mean, var, dev, inv, eps = sb("mean", [P, G]), sb("var", [P, G]), sb("dev", [P, G]), sb("inv", [P, G]), sb("eps", [P, 1])
        ht = sb("ht", [P, GN])
        hd = sb("hd", [P, G, D])
        ps_o, ps_h, ps_m = pb("ps_o"), pb("ps_h"), pb("ps_m")
        (w_in, x_in, d_in, y_done, t_done, y_free, t_free, epsilon, s_att, s_out, s_x1, s_sum, s_mean, s_cen,
         s_sq, s_var, s_dev, s_inv, s_nrm, s_relu, s_y, s_turned, s_ht, s_hd, s_hdc) = (sem(k) for k in (
             "w_in x_in d_in y_done t_done y_free t_free eps att out x1 sum mean cen sq var dev inv nrm relu y turned ht hd hdc").split())
        block = ctx.enter_context(nc.Block())

        @block.sync
        def _(sp):
            def load_den(g):
                sp.dma_start(inv_den[:, :, :], rden[:, bass.ds(g * GN, GN)].rearrange("(o t) n -> o t n", o=1).to_broadcast([P, NT, GN])).then_inc(d_in, 16)

            load_den(0)
            sp.dma_start(w[:, :, :], a["L0_gnn_W"].rearrange("t i o -> i t o")).then_inc(w_in, 16)
            sp.dma_start(bias[:, :], a["L0_gnn_bias"][:, :]).then_inc(w_in, 16)
            sp.dma_start(dw[:, :], a["L1_gnn_dW"][:, :]).then_inc(w_in, 16)
            sp.dma_start(db[:, :], a["L1_gnn_db"].rearrange("(o f) -> o f", o=1)).then_inc(w_in, 16)
            sp.dma_start(x[:, :, :], a["x"][0, :, :, :]).then_inc(x_in, 16)
            with sp.Fori(0, GROUPS - 1) as g:
                sp.wait_ge(s_att, g + 1)
                load_den(g + 1)
                sp.wait_ge(s_y, g + 1)
                sp.dma_start(x[:, :, :], a["x"][bass.ds(g + 1, 1), :, :, :].rearrange("o p t f -> (o p) t f")).then_inc(x_in, 16)

        @block.gpsimd
        def _(pool):
            pool.sem_inc(t_free, 1)
            pool.sem_inc(y_free, 1)
            with pool.Fori(0, GROUPS) as g:
                pool.wait_ge(s_y, g + 1)
                pool.dma_start(ypre[bass.ds(g, 1), :, :, :].rearrange("o p t f -> (o p) t f"), y[:, :, :]).then_inc(y_done, 16)
                pool.wait_ge(y_done, 16 * g + 16)
                pool.sem_inc(y_free, 1)
                pool.wait_ge(s_hdc, g + 1)
                pool.dma_start(table[bass.ds(g * GN, GN), :].rearrange("(t p) r -> p t r", p=P), hd[:, :, :]).then_inc(t_done, 16)
                pool.wait_ge(t_done, 16 * g + 16)
                pool.sem_inc(t_free, 1)

        @block.tensor
        def _(pe):
            def project(g):
                pe.wait_ge(s_att, g + 1)
                for j in range(G):
                    for t in range(NT):
                        nc.tensor.matmul(ps_o[:, j * P:(j + 1) * P], att[:, t, j * P:(j + 1) * P], w[:, t, :], start=(t == 0), stop=False)
                    last = nc.tensor.matmul(ps_o[:, j * P:(j + 1) * P], h.ones[0:NT, :], bias[:, :], start=False, stop=True)
                last.then_inc(s_out, 1)

            def messages(g):
                pe.wait_ge(s_relu, g + 1)
                for j in range(G):
                    last = nc.tensor.transpose(ps_h[:, j * P:(j + 1) * P], nrm[:, j, :], h.ident)
                last.then_inc(s_turned, 1)
                pe.wait_ge(s_ht, g + 1)
                for j in range(G):
                    nc.tensor.matmul(ps_m[:, j * P:(j + 1) * P], ht[:, j * P:(j + 1) * P], dw[:, :], start=True, stop=False)
                    last = nc.tensor.matmul(ps_m[:, j * P:(j + 1) * P], h.ones[0:1, :], db[:, :], start=False, stop=True)
                last.then_inc(s_hd, 1)

            pe.wait_ge(w_in, 64)
            project(0)
            with pe.Fori(0, GROUPS - 1) as g:
                pe.wait_ge(s_x1, g + 1)
                project(g + 1)
                messages(g)
            messages(GROUPS - 1)

        @block.scalar
        def _(act):
            act.wait_ge(epsilon, 1)
            with act.Fori(0, GROUPS) as g:
                act.wait_ge(s_var, g + 1)
                nc.scalar.activation(dev[:, :], var[:, :], ACT.Sqrt, bias=eps[:, :], scale=1.0 / D).then_inc(s_dev, 1)
                act.wait_ge(s_turned, g + 1)
                nc.scalar.copy(ht[:, :], ps_h[:, 0:GN]).then_inc(s_ht, 1)
                act.wait_ge(s_hd, g + 1)
                act.wait_ge(t_free, g + 1)
                nc.scalar.copy(hd[:, :, :].rearrange("p t f -> p (t f)"), ps_m[:, 0:GN]).then_inc(s_hdc, 1)

        @block.vector
        def _(dve):
            def normalise_sums(g):
                dve.wait_ge(d_in, 16 * g + 16)
                nc.vector.tensor_tensor(att[:, :, :], acc[:, :, bass.ds(g * GN, GN)], inv_den[:, :, :], ALU.mult).then_inc(s_att, 1)

            def layer_norm(g, meanwhile):
                dve.wait_ge(x_in, 16 * g + 16)
                dve.wait_ge(s_out, g + 1)
                xf = x[:, :, :].rearrange("p t f -> p (t f)")
                nc.vector.tensor_tensor(xf, xf, ps_o[:, 0:GN], ALU.add).then_inc(s_x1, 1)
                dve.wait_ge(s_x1, g + 1)
                nc.vector.tensor_reduce(out=mean[:, :], in_=x[:, :, :], op=ALU.add, axis=AX.X).then_inc(s_sum, 1)
                meanwhile()
                dve.wait_ge(s_sum, g + 1)
                nc.vector.tensor_scalar(mean[:, :], mean[:, :], 1.0 / D, None, ALU.mult).then_inc(s_mean, 1)
                dve.wait_ge(s_mean, g + 1)
                nc.vector.tensor_tensor(xc[:, :, :], x[:, :, :], mean[:, :].unsqueeze(2).to_broadcast([P, G, D]), ALU.subtract).then_inc(s_cen, 1)
                dve.wait_ge(s_cen, g + 1)
                nc.vector.tensor_tensor(sq[:, :, :], xc[:, :, :], xc[:, :, :], ALU.mult).then_inc(s_sq, 1)
                dve.wait_ge(s_sq, g + 1)
                nc.vector.tensor_reduce(out=var[:, :], in_=sq[:, :, :], op=ALU.add, axis=AX.X).then_inc(s_var, 1)
                dve.wait_ge(s_dev, g + 1)
                nc.vector.reciprocal(inv[:, :], dev[:, :]).then_inc(s_inv, 1)
                dve.wait_ge(s_inv, g + 1)
                nc.vector.tensor_tensor(xc[:, :, :], xc[:, :, :], inv[:, :].unsqueeze(2).to_broadcast([P, G, D]), ALU.mult).then_inc(s_nrm, 1)
                dve.wait_ge(s_nrm, g + 1)
                nc.vector.tensor_scalar(nrm[:, :, :], xc[:, :, :], 0.0, None, ALU.max).then_inc(s_relu, 1)
                dve.wait_ge(s_relu, g + 1)
                dve.wait_ge(y_free, g + 1)
                nc.vector.tensor_tensor(y[:, :, :], x[:, :, :], nrm[:, :, :], ALU.add).then_inc(s_y, 1)

            nc.vector.memset(eps[:, :], EPS).then_inc(epsilon, 1)
            normalise_sums(0)
            with dve.Fori(0, GROUPS - 1) as g:
                layer_norm(g, lambda: normalise_sums(g + 1))
            layer_norm(GROUPS - 1, lambda: None)


def convolution_edges(nc, h, a, acc, table):
    with ExitStack() as ctx:
        sb = lambda name, shape, dt=fp32: ctx.enter_context(nc.sbuf_tensor("ce_" + name, shape, dt))
        pb = lambda name, n=1024: ctx.enter_context(nc.psum_tensor("ce_" + name, [P, n], fp32))
        sem = lambda name: ctx.enter_context(nc.semaphore("ce_" + name))
        H = UE // 2
        fw1, fb1, fw2, fb2 = sb("fw1", [RBF, D]), sb("fb1", [D, 1]), sb("fw2", [D, D]), sb("fb2", [P, D])
        idx = [sb(f"idx{s}", [P, CH], i32) for s in range(SL)]
        xg = sb("xg", [P, XS, CH, D])
        ea = sb("ea", [RBF, XS, UE])
        hid = sb("hid", [P, 2, UE])
        flt, msg = sb("flt", [P, CH, D]), sb("msg", [P, 2, CH, D])
        hot = sb("hot", [P, 2, CH, W])
        rel = sb("rel", [P, NU, CH])
        ps_h = pb("ps_h")
        ps_f = [pb(f"ps_f{b}") for b in range(2)]
        ps_a = [pb(f"ps_a{b}", 512) for b in range(2)]
        idx_in = [sem(f"idx_in{s}") for s in range(SL)]
        sem_landed = sem("landed")
        gathered = [sem(f"gathered{s}") for s in range(XS)]
        ea_in = [sem(f"ea_in{s}") for s in range(XS)]
        (w_in, xg_free, pool_turn, ea_free, steps, key_ready, begun, cleared, s_hid, s_act, s_flt, s_bias, s_hot, s_msg, s_sum, s_acc) = (
            sem("c_" + k) for k in "w_in xg_free pool_turn ea_free steps key_ready begun cleared hid act flt bias hot msg sum acc".split())
        block = ctx.enter_context(nc.Block())

        @block.sync
        def _(sp):
            sp.dma_start(fw1[:, :], a["L1_gnn_fW1"][:, :]).then_inc(w_in, 16)
            sp.dma_start(fb1[:, :], a["L1_gnn_fb1"].rearrange("(f o) -> f o", o=1)).then_inc(w_in, 16)
            sp.dma_start(fw2[:, :], a["L1_gnn_fW2"][:, :]).then_inc(w_in, 16)
            sp.dma_start(fb2[:, :], a["L1_gnn_fb2"].rearrange("(o f) -> o f", o=1).to_broadcast([P, D])).then_inc(w_in, 16)

            def attributes(r, i, s):
                n = (r * TURNS + i) * SL + s + 1
                sp.wait_ge(s_hid, n)
                sp.dma_start(ea[:, s % XS, :], a["edge_attr_50"][:, bass.ds((i * SL + s) * UE, UE)]).then_inc(ea_in[s % XS], 16)
            load_indices(sp, a, h, idx, idx_in, gathered, sem_landed, attributes)

        @block.scalar
        def _(act):
            act.wait_ge(w_in, 64)
            with act.Fori(0, pass_count(act, h)) as r:
                def turn(i, first):
                    for s in range(SL):
                        n, b = (r * TURNS + i) * SL + s + 1, s % 2
                        act.wait_ge(s_hid, n + XS)
                        if not (first and s < 2):
                            act.wait_ge(s_flt, n - 2)
                        nc.scalar.activation(hid[:, b, :].rearrange("p (k e) -> p k e", k=2), ps_h[:, :].rearrange("p (k e) -> p k e", k=2)[:, :, 0:H],
                                             ACT.Silu, bias=fb1[:, :]).then_inc(s_act, 1)
                turns(act, turn)

        @block.gpsimd
        def _(pool):
            gather_units(pool, h, table, xg, D, idx, idx_in, gathered, s_msg, pool_turn)

        @block.tensor
        def _(pe):
            pe.sem_inc(s_hid, XS)
            pe.wait_ge(w_in, 64)
            with pe.Fori(0, pass_count(pe, h)) as r:
                def filters(n, s):
                    b = s % 2
                    pe.wait_ge(s_act, n)
                    for c in range(CH):
                        last = nc.tensor.matmul(ps_f[b][:, c * D:(c + 1) * D], hid[:, b, c * P:(c + 1) * P], fw2[:, :], start=True, stop=True)
                    last.then_inc(s_flt, 1)

                def sums(n, s):
                    b = s % 2
                    pe.wait_ge(s_msg, n + XS)
                    for c in range(CH):
                        last = nc.tensor.matmul(ps_a[b][:, 0:W], msg[:, b, c, :], hot[:, b, c, :], start=(c == 0), stop=(c == CH - 1))
                    last.then_inc(s_sum, 1)

                def turn(i, first):
                    for s in range(SL):
                        n = (r * TURNS + i) * SL + s + 1
                        if not (first and s < 1):
                            pe.wait_ge(s_act, n - 1)
                        pe.wait_ge(ea_in[s % XS], 16 * (PER * (r * TURNS + i) + s // XS + 1))
                        for k in range(2):
                            last = nc.tensor.matmul(ps_h[:, k * 512:k * 512 + H], fw1[:, :], ea[:, s % XS, k * H:(k + 1) * H], start=True, stop=True)
                        last.then_inc(s_hid, 1)
                        if not (first and s < 2):
                            sums(n - 2, s)
                        if not (first and s < 1):
                            filters(n - 1, s - 1)
                turns(pe, turn)
                n = (r + 1) * NU
                sums(n - 1, SL - 2)
                filters(n, SL - 1)
                sums(n, SL - 1)

        @block.vector
        def _(dve):
            dve.sem_inc(s_msg, XS)
            nc.vector.memset(h.sweep[:, :], 0.0).then_inc(cleared, 1)
            nc.vector.memset(acc[:, :], 0.0).then_inc(cleared, 1)
            dve.wait_ge(cleared, 2)
            dve.wait_ge(w_in, 64)
            with dve.Fori(0, pass_count(dve, h)) as r:
                def one_hot(unit, s):
                    b = s % 2
                    keys = h.key[:, bass.ds(unit, 1), :].rearrange("p o c -> p (o c)")
                    nc.vector.tensor_tensor(hot[:, b, :, :], h.iota[:, 0:W].unsqueeze(1).to_broadcast([P, CH, W]),
                                            keys.unsqueeze(2).to_broadcast([P, CH, W]), ALU.is_equal).then_inc(s_hot, 1)

                def messages(n, s, count):
                    b = s % 2
                    dve.wait_ge(s_flt, n)
                    nc.vector.tensor_tensor(flt[:, :, :], ps_f[b][:, 0:CH * D].rearrange("p (c f) -> p c f", c=CH),
                                            fb2[:, :].unsqueeze(1).to_broadcast([P, CH, D]), ALU.add).then_inc(s_bias, 1)
                    dve.wait_ge(s_bias, n)
                    dve.wait_ge(gathered[s % XS], GI * count)
                    nc.vector.tensor_tensor(msg[:, b, :, :], flt[:, :, :], xg[:, s % XS, :, :], ALU.mult).then_inc(s_msg, 1)

                def merge(n, s, base, fresh):
                    dve.wait_ge(s_sum, n)
                    if not fresh:
                        dve.wait_ge(s_acc, n - 1)
                    win = bass.ds(base, W)
                    nc.vector.tensor_tensor(acc[:, win], acc[:, win], ps_a[s % 2][:, 0:W], ALU.add).then_inc(s_acc, 1)

                def turn(i, first):
                    back = 0 if first else 2
                    base = bases(nc, mybir.EngineType.DVE, h, i * SL - back, SL + back)
                    for s in range(SL):
                        t = r * TURNS + i
                        n, v = t * SL + s + 1, (s - 1) % SL
                        if not (first and s < 1):
                            one_hot(i * SL + s - 1, v)
                        if not (first and s < 2):
                            merge(n - 2, s, base[s + back - 2], first and s == 2)
                        if not (first and s < 1):
                            messages(n - 1, v, PER * t + v // XS + 1 - (PER if s == 0 else 0))

                start_pass(nc, dve, h, r, steps, key_ready, begun, rel[:, :, :])
                turns(dve, turn)
                n = (r + 1) * NU
                base = bases(nc, mybir.EngineType.DVE, h, NU - 2, 2)
                one_hot(NU - 1, SL - 1)
                merge(n - 1, SL - 2, base[0], False)
                messages(n, SL - 1, PER * TURNS * (r + 1))
                merge(n, SL - 1, base[1], False)
                dve.wait_ge(s_acc, n)


def finish(nc, h, a, acc, ypre, out):
    with ExitStack() as ctx:
        sb = lambda name, shape, dt=fp32: ctx.enter_context(nc.sbuf_tensor("fi_" + name, shape, dt))
        pb = lambda name: ctx.enter_context(nc.psum_tensor("fi_" + name, [P, 1024], fp32))
        sem = lambda name: ctx.enter_context(nc.semaphore("fi_" + name))
        w1, b1, w2, b2 = sb("w1", [D, D]), sb("b1", [D, 1]), sb("w2", [D, D]), sb("b2", [1, D])
        hid, y = sb("hid", [P, GN]), sb("y", [P, G, D])
        ps_u, ps_y = pb("ps_u"), pb("ps_y")
        (w_in, y_in, y_free, out_done, s_u, s_hid, s_v, s_y) = (sem("u_" + k) for k in "w_in y_in y_free out_done u hid v y".split())
        block = ctx.enter_context(nc.Block())

        @block.sync
        def _(sp):
            sp.sem_inc(y_free, 1)
            sp.dma_start(w1[:, :], a["L1_gnn_uW1"][:, :]).then_inc(w_in, 16)
            sp.dma_start(b1[:, :], a["L1_gnn_ub1"].rearrange("(f o) -> f o", o=1)).then_inc(w_in, 16)
            sp.dma_start(w2[:, :], a["L1_gnn_uW2"][:, :]).then_inc(w_in, 16)
            sp.dma_start(b2[:, :], a["L1_gnn_ub2"].rearrange("(o f) -> o f", o=1)).then_inc(w_in, 16)
            with sp.Fori(0, GROUPS) as g:
                sp.wait_ge(y_free, g + 1)
                sp.dma_start(y[:, :, :], ypre[bass.ds(g, 1), :, :, :].rearrange("o p t f -> (o p) t f")).then_inc(y_in, 16)
                sp.wait_ge(s_y, g + 1)
                sp.dma_start(out[bass.ds(g * GN, GN), :].rearrange("(t p) f -> p t f", p=P), y[:, :, :]).then_inc(out_done, 16)
                sp.wait_ge(out_done, 16 * g + 16)
                sp.sem_inc(y_free, 1)

        @block.tensor
        def _(pe):
            pe.wait_ge(w_in, 64)
            with pe.Fori(0, GROUPS) as g:
                for k in range(2):
                    last = nc.tensor.matmul(ps_u[:, k * 512:k * 512 + GN // 2], w1[:, :], acc[:, bass.ds(g * GN + k * (GN // 2), GN // 2)], start=True, stop=True)
                last.then_inc(s_u, 1)
                pe.wait_ge(s_hid, g + 1)
                for j in range(G):
                    nc.tensor.matmul(ps_y[:, j * P:(j + 1) * P], hid[:, j * P:(j + 1) * P], w2[:, :], start=True, stop=False)
                    last = nc.tensor.matmul(ps_y[:, j * P:(j + 1) * P], h.ones[0:1, :], b2[:, :], start=False, stop=True)
                last.then_inc(s_v, 1)
                pe.wait_ge(s_y, g + 1)

        @block.scalar
        def _(act):
            act.wait_ge(w_in, 64)
            with act.Fori(0, GROUPS) as g:
                act.wait_ge(s_u, g + 1)
                nc.scalar.activation(hid[:, :].rearrange("p (k n) -> p k n", k=2), ps_u[:, :].rearrange("p (k n) -> p k n", k=2)[:, :, 0:GN // 2],
                                     ACT.Silu, bias=b1[:, :]).then_inc(s_hid, 1)

        @block.vector
        def _(dve):
            with dve.Fori(0, GROUPS) as g:
                dve.wait_ge(y_in, 16 * g + 16)
                dve.wait_ge(s_v, g + 1)
                yf = y[:, :, :].rearrange("p t f -> p (t f)")
                nc.vector.tensor_tensor(yf, yf, ps_y[:, 0:GN], ALU.add).then_inc(s_y, 1)


def program(nc, a, out):
    table0 = nc.dram_tensor("table0", (NP, ROW), fp32).ap()
    table1 = nc.dram_tensor("table1", (NP, D), fp32).ap()
    den = nc.dram_tensor("den", (NT, NP), fp32).ap()
    rden = nc.dram_tensor("rden", (NT, NP), fp32).ap()
    ypre = nc.dram_tensor("ypre", (GROUPS, P, G, D), fp32).ap()
    with ExitStack() as ctx:
        h = Held(nc, ctx)
        with ExitStack() as att:
            acc = att.enter_context(nc.sbuf_tensor("att_acc", [P, NT, NW], fp32))
            with nc.sbuf_tensor("state", [P, NT, NW], fp32) as state, nc.sbuf_tensor("typ", [P, NU, CH], bf16) as typ:
                prepare_edges(nc, h, a, typ)
                prepare_nodes(nc, h, a, acc, state, table0)
                attention_edges(nc, h, a, acc, state, typ, table0)
                invert_denominators(nc, state, den, rden)
            finish_attention(nc, h, a, acc, rden, table1, ypre)
        acc = ctx.enter_context(nc.sbuf_tensor("conv_acc", [P, NW], fp32))
        convolution_edges(nc, h, a, acc, table1)
        finish(nc, h, a, acc, ypre, out)


def kernel(**inputs):
    import concourse.bacc as bacc
    from concourse.bass_utils import run_bass_kernel_spmd

    def padded(v, n, fill):
        return np.concatenate([v, np.full((n - v.shape[0],) + v.shape[1:], fill, v.dtype)])

    def by_unit(v, fill):
        return padded(np.asarray(v), EP, fill).reshape(NU, CH, P).transpose(0, 2, 1)

    given = {k: np.asarray(v) for k, v in inputs.items()}
    arrays = {k: given[k] for k in (
        "L0_gnn_emb_table", "L0_gnn_W", "L0_gnn_bias", "L1_gnn_fW1", "L1_gnn_fb1", "L1_gnn_fW2", "L1_gnn_fb2",
        "L1_gnn_dW", "L1_gnn_db", "L1_gnn_uW1", "L1_gnn_ub1", "L1_gnn_uW2", "L1_gnn_ub2")}
    arrays["cst"] = constants()
    arrays["x"] = padded(given["x"], NP, 0).reshape(GROUPS, G, P, D).transpose(0, 2, 1, 3)
    arrays["node_type_3"] = padded(given["node_type_3"], NP, 0).reshape(1, NP)
    arrays["src"] = by_unit(given["src"], 0)
    arrays["dst"] = by_unit(given["dst"], N).transpose(1, 0, 2)
    arrays["edge_type_3"] = by_unit(given["edge_type_3"], 0).transpose(1, 0, 2)
    arrays["edge_attr_50"] = padded(given["edge_attr_50"], EP, 0).T
    arrays["w_t"] = given["L0_gnn_W"].transpose(2, 0, 1)
    arrays["att"] = np.concatenate([given["L0_gnn_att_src"], given["L0_gnn_att_dst"]]).T

    nc = bacc.Bacc("TRN2", target_bir_lowering=False, num_devices=1)
    arrays = {"in_" + k: np.ascontiguousarray(v) for k, v in arrays.items()}
    a = {k[3:]: nc.dram_tensor(k, v.shape, mybir.dt.from_np(v.dtype), kind="ExternalInput").ap() for k, v in arrays.items()}
    out = nc.dram_tensor("out_x", (NP, D), fp32, kind="ExternalOutput").ap()
    program(nc, a, out)
    r = run_bass_kernel_spmd(nc, [arrays], core_ids=[0])
    return r.results[0]["out_x"][:N]
```

```python
import numpy as np
import concourse.bass as bass
from concourse import mybir
from contextlib import ExitStack

N, D, NT, RBF = 6250, 128, 3, 50
E = 206250
P = 128
CH = 6
UE = CH * P
SL = 6
NU = -(-E // (UE * SL)) * SL
TURNS = NU // SL
EP = NU * UE
XS = 6
PER = SL // XS
GI = 16 * CH
STEPS = 8
W = 32
KEYS = NT * W
G = 7
TILES = -(-N // P)
GROUPS = TILES // G
GN = G * P
NP = TILES * P
NW = NP + W
PASSES = NP // W
ROW = 132
TQ = NU // 3
SLOPE = 0.2
EPS = 1e-5
BIG = 1e30
assert TILES % G == 0 and TQ <= P and GN // 2 <= 512

fp32, bf16 = mybir.dt.float32, mybir.dt.bfloat16
i32, u16 = mybir.dt.int32, mybir.dt.uint16
ALU, ACT, AX = mybir.AluOpType, mybir.ActivationFunctionType, mybir.AxisListType


def gather(eng, out, table, idx, done):
    eng.indirect_dma_start(out=out, out_offset=None, in_=table[:, :],
                           in_offset=bass.IndirectOffsetOnAxis(ap=idx, axis=0)).then_inc(done, 16)


class Held:

    def __init__(self, nc, ctx):
        sb = lambda name, shape, dt=fp32: ctx.enter_context(nc.sbuf_tensor(name, shape, dt))
        self.cst = sb("cst", [P, 4 * P + KEYS + 1])
        c = self.cst
        self.ident = c[:, 0:P]
        self.ones = c[:, P:2 * P]
        self.less_row32 = c[:, 2 * P:3 * P]
        self.slope = c[:, 3 * P:4 * P]
        self.iota = c[:, 4 * P:4 * P + KEYS]
        self.kind = c[:, 4 * P + KEYS:]
        self.rows_w = sb("rows_w", [P, NT, 64])
        self.dst = sb("dst", [P, NU, CH], u16)
        self.key = sb("key", [P, NU, CH], bf16)
        self.ubase = sb("ubase", [P, NU])
        self.base = sb("base", [P, NU])
        self.base_i = sb("base_i", [P, NU], i32)
        self.wide = sb("wide", [P, 1])
        self.narrow = sb("narrow", [P, 1])
        self.passes = sb("passes", [P, 1], i32)
        self.sweep = sb("sweep", [P, 1])


def constants():
    c = np.zeros((P, 4 * P + KEYS + 1), np.float32)
    c[:, 0:P] = np.eye(P)
    c[:, P:2 * P] = 1
    c[32, 2 * P:3 * P] = -1
    c[:, 3 * P:4 * P] = SLOPE
    c[:, 4 * P:4 * P + KEYS] = np.arange(KEYS)
    c[:, 4 * P + KEYS] = np.arange(P)
    return c


def node_groups(body):
    def run(eng):
        body(0, 0, True)
        with eng.Fori(0, (GROUPS - 1) // 2) as i:
            body(2 * i + 1, 1, False)
            body(2 * i + 2, 0, False)
    return run


def prepare(nc, h, a, acc, state, typ, table):
    with ExitStack() as ctx:
        sb = lambda name, shape, dt=fp32: ctx.enter_context(nc.sbuf_tensor("pr_" + name, shape, dt))
        pb = lambda name, n=1024: ctx.enter_context(nc.psum_tensor("pr_" + name, [P, n], fp32))
        sem = lambda name: ctx.enter_context(nc.semaphore("pr_" + name))
        raw = sb("raw", [P, NU, CH], i32)
        lim, col = sb("lim", [P, 2, NU]), sb("col", [P, 2, 3])
        span, top = sb("span", [P, NU]), sb("top", [P, 1])
        wt, att, emb = sb("wt", [P, NT, D]), sb("att", [P, 2 * NT]), sb("emb", [3, D])
        score = sb("score", [P, 2 * NT])
        nt_i, nt1h = sb("nt_i", [3, GN], i32), sb("nt1h", [3, GN])
        x, relu, rows, xt = sb("x", [P, 2, G, D]), sb("relu", [P, G, D]), sb("rows", [P, 2, G, ROW]), sb("xt", [P, GN])
        stats, moments = sb("stats", [P, G, 6]), sb("moments", [P, G, 2])
        dev, inv, shift, eps = sb("dev", [P, G]), sb("inv", [P, G]), sb("shift", [P, G]), sb("eps", [P, 1])
        ps_e, ps_x, ps_s, ps_l = pb("ps_e"), pb("ps_x"), pb("ps_s", 512), pb("ps_l", 1024)
        (cst_in, dst_in, typ_in, w_in, att_in, emb_in, nt_in) = (sem(k) for k in "cst_in dst_in typ_in w_in att_in emb_in nt_in".split())
        x_in, out_done, rows_free = ([sem(f"{k}{s}") for s in range(2)] for k in ("x_in", "out_done", "rows_free"))
        (s_lims, s_dst, s_turned, s_cols, s_spread, s_steps, s_weights, s_score, s_const, s_filled, s_onehot, s_emb, s_stats, s_var, s_dev,
         s_inv, s_shift, s_relu, s_feat, s_turn, s_xt, s_scores, s_acc, s_as, s_begun, s_blank) = (sem(k) for k in (
             "lims dst turned cols spread steps weights score const filled onehot emb stats var dev inv shift relu feat turn xt scores acc as begun blank").split())
        block = ctx.enter_context(nc.Block())

        @block.sync
        def _(sp):
            def types(g):
                sp.dma_start(nt_i[:, :], a["node_type_3"][0:1, bass.ds(g * GN, GN)].to_broadcast([3, GN])).then_inc(nt_in, 16)

            sp.dma_start(x[:, 0, :, :], a["x"][0, :, :, :]).then_inc(x_in[0], 16)
            types(0)
            sp.dma_start(emb[:, :], a["L0_gnn_emb_table"][:, :]).then_inc(emb_in, 16)
            sp.dma_start(h.cst[:, :], a["cst"][:, :]).then_inc(cst_in, 16)
            sp.dma_start(raw[:, :, :], a["dst"][:, :, :]).then_inc(dst_in, 16)
            sp.dma_start(x[:, 1, :, :], a["x"][1, :, :, :]).then_inc(x_in[1], 16)
            sp.dma_start(wt[:, :, :], a["w_t"][:, :, :]).then_inc(w_in, 16)
            sp.dma_start(att[:, :], a["att"][:, :]).then_inc(att_in, 16)
            sp.wait_ge(s_onehot, 1)
            types(1)
            sp.wait_ge(s_relu, 1)
            sp.dma_start(x[:, 0, :, :], a["x"][2, :, :, :]).then_inc(x_in[0], 16)
            sp.wait_ge(s_dst, 2)
            sp.dma_start(raw[:, :, :], a["edge_type_3"][:, :, :]).then_inc(typ_in, 16)
            with sp.Fori(0, (GROUPS - 3) // 2) as i:
                for k in range(2):
                    g, s = 2 * i + 1 + k, 1 - k
                    sp.wait_ge(s_onehot, g + 1)
                    types(g + 1)
                    sp.wait_ge(s_relu, g + 1)
                    sp.dma_start(x[:, s, :, :], a["x"][bass.ds(g + 2, 1), :, :, :].rearrange("o p t f -> (o p) t f")).then_inc(x_in[s], 16)
            sp.wait_ge(s_onehot, GROUPS - 1)
            types(GROUPS - 1)

        @block.gpsimd
        def _(pool):
            pool.sem_inc(rows_free[0], 1)
            pool.sem_inc(rows_free[1], 1)
            for k, (part, value) in enumerate(((state[0:64, :, NP:NW], 0.0), (acc[:, :, NP:NW], 0.0), (state[64:P, :, :], 1.0))):
                if k:
                    pool.wait_ge(s_filled, k)
                pool.memset(part, value).then_inc(s_filled, 1)
            pool.wait_ge(s_filled, 3)

            def store(g, s, count, first):
                if not first:
                    pool.wait_ge(out_done[1 - s], 16 * count)
                    pool.sem_inc(rows_free[1 - s], 1)
                pool.wait_ge(s_feat, g + 1)
                pool.wait_ge(s_as, g + 1)
                pool.dma_start(table[bass.ds(g * GN, GN), :].rearrange("(t p) r -> p t r", p=P), rows[:, s, :, :]).then_inc(out_done[s], 16)

            store(0, 0, 0, True)
            with pool.Fori(0, (GROUPS - 1) // 2) as i:
                store(2 * i + 1, 1, i + 1, False)
                store(2 * i + 2, 0, i + 1, False)
            pool.wait_ge(out_done[0], 16 * (GROUPS // 2 + 1))

        @block.tensor
        def _(pe):
            def embeddings(g):
                pe.wait_ge(s_onehot, g + 1)
                for t in range(G):
                    last = nc.tensor.matmul(ps_e[:, t * P:(t + 1) * P], nt1h[:, t * P:(t + 1) * P], emb[:, :], start=True, stop=True)
                last.then_inc(s_emb, 1)

            def turn(g, s):
                pe.wait_ge(s_feat, g + 1)
                for t in range(G):
                    last = nc.tensor.transpose(ps_x[:, t * P:(t + 1) * P], rows[:, s, t, 0:D], h.ident)
                last.then_inc(s_turn, 1)

            def scores(g, first):
                pe.wait_ge(s_xt, g + 1)
                if not first:
                    pe.wait_ge(s_as, g)
                for t in range(G):
                    last = nc.tensor.matmul(ps_s[:, 8 + NT * t:8 + NT * t + NT], xt[:, t * P:(t + 1) * P], score[:, 0:NT], start=True, stop=True)
                last.then_inc(s_scores, 1)

            pe.wait_ge(emb_in, 16)
            embeddings(0)
            pe.wait_ge(w_in, 16)
            pe.wait_ge(att_in, 16)
            for t in range(NT):
                for k in range(2):
                    c = k * NT + t
                    last = nc.tensor.matmul(ps_s[:, c:c + 1], wt[:, t, :], att[:, c:c + 1], start=True, stop=True)
            last.then_inc(s_weights, 1)
            pe.wait_ge(cst_in, 16)
            pe.wait_ge(s_lims, 1)
            for k in range(2):
                for q in range(3):
                    last = nc.tensor.transpose(ps_l[0:TQ, k * 512 + q * P:k * 512 + (q + 1) * P], lim[:, k, q * TQ:(q + 1) * TQ], h.ident)
            last.then_inc(s_turned, 1)
            turn(0, 0)
            embeddings(1)
            pe.wait_ge(s_score, 1)
            scores(0, True)
            pe.wait_ge(s_cols, 2)
            for k in range(2):
                for q in range(3):
                    last = nc.tensor.matmul(ps_l[:, k * 512 + q * TQ:k * 512 + (q + 1) * TQ],
                                            col[0:TQ, k, q:q + 1].to_broadcast([TQ, P]), h.ident[0:TQ, 0:TQ],
                                            start=True, stop=True)
            last.then_inc(s_spread, 1)
            with pe.Fori(0, (GROUPS - 3) // 2) as i:
                for k in range(2):
                    g = 2 * i + 1 + k
                    turn(g, 1 - k)
                    embeddings(g + 1)
                    scores(g, False)
            turn(GROUPS - 2, (GROUPS - 2) % 2)
            embeddings(GROUPS - 1)
            scores(GROUPS - 2, False)
            turn(GROUPS - 1, (GROUPS - 1) % 2)
            scores(GROUPS - 1, False)

        @block.scalar
        def _(act):
            def finish_group(g, s):
                act.wait_ge(s_xt, g + 1)
                nc.scalar.copy(acc[:, :, bass.ds(g * GN, GN)], xt[:, :].unsqueeze(1).to_broadcast([P, NT, GN])).then_inc(s_acc, 1)
                act.wait_ge(s_scores, g + 1)
                nc.scalar.copy(rows[:, s, :, D:D + NT], ps_s[:, 8:8 + NT * G].rearrange("p (t k) -> p t k", k=NT)).then_inc(s_as, 1)

            def group(g, s, first):
                act.wait_ge(s_var, g + 1)
                nc.scalar.activation(dev[:, :], moments[:, :, 1], ACT.Sqrt, bias=eps[:, :]).then_inc(s_dev, 1)
                act.wait_ge(s_shift, g + 1)
                for t in range(G):
                    last = nc.scalar.activation(relu[:, t, :], x[:, s, t, :], ACT.Relu, bias=shift[:, t:t + 1], scale=inv[:, t:t + 1])
                last.then_inc(s_relu, 1)
                if not first:
                    finish_group(g - 1, 1 - s)
            act.wait_ge(s_const, 2)
            node_groups(group)(act)
            finish_group(GROUPS - 1, (GROUPS - 1) % 2)

        @block.vector
        def _(dve):
            def normalised(g, s, count, first):
                dve.wait_ge(s_relu, g + 1)
                dve.wait_ge(s_emb, g + 1)
                dve.wait_ge(rows_free[s], count + 1)
                nc.vector.tensor_tensor(rows[:, s, :, 0:D], relu[:, :, :], ps_e[:, 0:GN].rearrange("p (t f) -> p t f", t=G), ALU.add).then_inc(s_feat, 1)

            def turned(g, first):
                dve.wait_ge(s_turn, g + 1)
                if not first:
                    dve.wait_ge(s_acc, g)
                    dve.wait_ge(s_scores, g)
                nc.vector.tensor_copy(xt[:, :], ps_x[:, 0:GN]).then_inc(s_xt, 1)

            def group(g, s, count, before, first=False):
                if before:
                    normalised(g - 1, *before)
                dve.wait_ge(nt_in, 16 * g + 16)
                if not first:
                    dve.wait_ge(s_emb, g)
                nc.vector.tensor_scalar(nt1h[:, :], nt_i[:, :], h.kind[0:3, :], None, ALU.is_equal).then_inc(s_onehot, 1)
                dve.wait_ge(x_in[s], 16 * count + 16)
                for t in range(G):
                    last = nc.vector.bn_stats(stats[:, t, :], x[:, s, t, :])
                last.then_inc(s_stats, 1)
                dve.wait_ge(s_stats, g + 1)
                dve.sem_inc(s_begun, 1)
                for t in range(G):
                    last = nc.vector.bn_aggr(moments[:, t, :], stats[:, t, :])
                last.then_inc(s_var, 1)
                dve.wait_ge(s_dev, g + 1)
                nc.vector.reciprocal(inv[:, :], dev[:, :]).then_inc(s_inv, 1)
                dve.wait_ge(s_inv, g + 1)
                nc.vector.scalar_tensor_tensor(out=shift[:, :], in0=moments[:, :, 0], scalar=-1.0, in1=inv[:, :],
                                               op0=ALU.mult, op1=ALU.mult).then_inc(s_shift, 1)
                if before:
                    turned(g - 1, before[-1])

            nc.vector.memset(h.sweep[:, :], 0.0).then_inc(s_const, 1)
            nc.vector.memset(eps[:, :], EPS).then_inc(s_const, 1)
            nc.vector.memset(rows[:, :, :, D + NT:ROW], 0.0)
            nc.vector.memset(h.rows_w[:, :, :], 0.0).then_inc(s_blank, 1)
            dve.wait_ge(cst_in, 16)
            group(0, 0, 0, None, True)
            dve.wait_ge(dst_in, 16)
            nc.vector.tensor_reduce(out=lim[:, 0, :], in_=raw[:, :, :], op=ALU.min, axis=AX.X).then_inc(s_dst, 1)
            nc.vector.tensor_reduce(out=lim[:, 1, :], in_=raw[:, :, :], op=ALU.max, axis=AX.X).then_inc(s_lims, 1)
            nc.vector.tensor_copy(h.dst[:, :, :], raw[:, :, :]).then_inc(s_dst, 1)
            dve.wait_ge(s_weights, 1)
            nc.vector.tensor_copy(score[:, :], ps_s[:, 0:2 * NT]).then_inc(s_score, 1)
            dve.wait_ge(s_score, 1)
            dve.wait_ge(s_blank, 1)
            nc.vector.tensor_copy(h.rows_w[:, :, 0], score[:, NT:2 * NT])
            nc.vector.tensor_tensor(h.rows_w[:, :, 32], score[:, 0:NT], score[:, NT:2 * NT], ALU.add)
            group(1, 1, 0, (0, 0, True))
            dve.wait_ge(s_turned, 1)
            for k, op in enumerate((ALU.min, ALU.max)):
                nc.vector.tensor_reduce(out=col[0:TQ, k, :], in_=ps_l[0:TQ, k * 512:k * 512 + 3 * P].rearrange("u (q p) -> u q p", q=3),
                                        op=op, axis=AX.X).then_inc(s_cols, 1)
            dve.wait_ge(typ_in, 16)
            nc.vector.tensor_copy(typ[:, :, :], raw[:, :, :])
            with dve.Fori(0, (GROUPS - 3) // 2) as i:
                group(2 * i + 2, 0, i + 1, (1, i, False))
                group(2 * i + 3, 1, i + 1, (0, i + 1, False))
            g = GROUPS - 1
            group(g, 0, g // 2, (1, g // 2 - 1, False))
            dve.wait_ge(s_spread, 1)
            nc.vector.tensor_copy(h.ubase[:, :], ps_l[:, 0:NU]).then_inc(s_steps, 1)
            dve.wait_ge(s_steps, 1)
            nc.vector.tensor_tensor(span[:, :], ps_l[:, 512:512 + NU], h.ubase[:, :], ALU.subtract).then_inc(s_steps, 1)
            normalised(g, 0, g // 2, False)
            dve.wait_ge(s_steps, 2)
            nc.vector.tensor_reduce(out=top[:, :], in_=span[:, :], op=ALU.max, axis=AX.X).then_inc(s_steps, 1)
            dve.wait_ge(s_steps, 3)
            nc.vector.tensor_scalar(h.wide[:, :], top[:, :], W - 0.5, None, ALU.is_gt).then_inc(s_steps, 1)
            dve.wait_ge(s_steps, 4)
            nc.vector.tensor_scalar(h.narrow[:, :], h.wide[:, :], -1.0, 1.0, ALU.mult, ALU.add)
            nc.vector.tensor_scalar(h.passes[:, :], h.wide[:, :], PASSES - 1.0, 1.0, ALU.mult, ALU.add)
            turned(g, False)


def start_pass(nc, dve, h, r, steps, key_ready, begun, rel, typ=None):
    done = [0]

    def link(ins):
        done[0] += 1
        ins.then_inc(steps, 1)
        dve.wait_ge(steps, r * STEPS + done[0])

    link(nc.vector.tensor_tensor(h.base[:, :], h.ubase[:, :], h.narrow[:, :].to_broadcast([P, NU]), ALU.mult))
    link(nc.vector.tensor_tensor(h.base[:, :], h.base[:, :], h.sweep[:, :].to_broadcast([P, NU]), ALU.add))
    nc.vector.tensor_copy(h.base_i[:, :], h.base[:, :])
    link(nc.vector.tensor_tensor(rel, h.dst[:, :, :], h.base[:, :].unsqueeze(2).to_broadcast([P, NU, CH]), ALU.subtract))
    link(nc.vector.scalar_tensor_tensor(out=h.sweep[:, :], in0=h.wide[:, :], scalar=float(W), in1=h.sweep[:, :], op0=ALU.mult, op1=ALU.add))
    link(nc.vector.tensor_scalar(h.key[:, :, :], rel, -0.5, None, ALU.is_gt))
    link(nc.vector.scalar_tensor_tensor(out=h.key[:, :, :], in0=rel, scalar=W - 0.5, in1=h.key[:, :, :], op0=ALU.is_lt, op1=ALU.mult))
    if typ is not None:
        link(nc.vector.scalar_tensor_tensor(out=rel, in0=typ[:, :, :], scalar=float(W), in1=rel, op0=ALU.mult, op1=ALU.add))
    link(nc.vector.scalar_tensor_tensor(out=rel, in0=rel, scalar=1.0, in1=h.key[:, :, :], op0=ALU.add, op1=ALU.mult))
    if typ is None:
        done[0] += 1
        dve.sem_inc(steps, 1)
    assert done[0] == STEPS
    nc.vector.tensor_scalar(h.key[:, :, :], rel, -1.0, None, ALU.add).then_inc(key_ready, 1)
    dve.wait_ge(key_ready, r + 1)
    dve.sem_inc(begun, 1)


def pass_count(eng, h):
    return eng.value_load(h.passes[0:1, 0:1], min_val=1, max_val=PASSES)


def bases(nc, engine, h, first, count):
    return nc.values_load_multi_w_load_instructions(h.base_i[0:1, bass.ds(first, count)], engines=[engine],
                                                    min_val=0, max_val=N,
                                                    skip_runtime_bounds_check_because="a destination is a node, a padding edge's is N")[1]


def turns(eng, body):
    body(0, True)
    with eng.Fori(1, TURNS) as i:
        body(i, False)


def load_indices(sp, a, h, idx, idx_in, gathered, landed, also=lambda r, i, s: None, early=lambda: None):
    for s in range(SL):
        sp.dma_start(idx[s][:, :], a["src"][s, :, :]).then_inc(idx_in[s], 16)
    early()
    passes = pass_count(sp, h)
    with sp.Fori(0, passes) as r:
        with sp.Fori(0, TURNS - 1) as i:
            for s in range(SL):
                also(r, i, s)
                sp.wait_ge(gathered[s % XS], GI * (PER * (r * TURNS + i) + s // XS + 1))
                sp.dma_start(idx[s][:, :], a["src"][bass.ds((i + 1) * SL + s, 1), :, :].rearrange("o p c -> (o p) c")).then_inc(idx_in[s], 16)
        for s in range(SL):
            also(r, TURNS - 1, s)
            sp.wait_ge(gathered[s % XS], GI * (PER * (r * TURNS + TURNS - 1) + s // XS + 1))
            sp.dma_start(idx[s][:, :], a["src"][s, :, :]).then_inc(idx_in[s], 16)
    for s in range(SL):
        sp.wait_ge(idx_in[s], 16 * (passes * TURNS + 1))
    sp.sem_inc(landed, 1)


def gather_units(pool, h, table, xg, width, idx, idx_in, gathered, xg_free, pool_turn):
    with pool.Fori(0, pass_count(pool, h)) as r:
        with pool.Fori(0, TURNS) as i:
            for s in range(SL):
                pool.wait_ge(idx_in[s], 16 * (r * TURNS + i + 1))
                pool.wait_ge(xg_free, (r * TURNS + i) * SL + s + 1)
                pool.sem_inc(pool_turn, 1)
                for c in range(CH):
                    gather(pool, xg[:, s % XS, c, 0:width], table, idx[s][:, c:c + 1], gathered[s % XS])


def attention_edges(nc, h, a, acc, state, typ, table, den):
    with ExitStack() as ctx:
        sb = lambda name, shape, dt=fp32: ctx.enter_context(nc.sbuf_tensor("ae_" + name, shape, dt))
        pb = lambda name: ctx.enter_context(nc.psum_tensor("ae_" + name, [P, 512], fp32))
        sem = lambda name: ctx.enter_context(nc.semaphore("ae_" + name))
        idx = [sb(f"idx{s}", [P, CH], i32) for s in range(SL)]
        xg = sb("xg", [P, XS, CH, ROW])
        oh3, pick = sb("oh3", [P, CH, NT], bf16), sb("pick", [P, CH, NT])
        sc, sc2 = sb("sc", [P, 2, CH]), sb("sc2", [P, 2, CH])
        off = sb("off", [P, 3, CH, KEYS], bf16)
        e = sb("e", [P, 3, CH * KEYS])
        masked = e[:, 2, :].rearrange("p (c k) -> p c k", c=CH)
        by_chunk = [e[:, b, :].rearrange("p (c k) -> p c k", c=CH) for b in range(2)]
        rel = e[:, :, :].rearrange("p a k -> p (a k)")[:, 0:NU * CH].rearrange("p (u c) -> p u c", c=CH)
        high, high_k = sb("high", [P, KEYS]), sb("high_k", [KEYS, 1])
        top, rise = sb("top", [64, KEYS]), sb("rise", [64, 2, KEYS])
        rescale = sb("rescale", [P, 2, KEYS])
        ps_t, ps_z = pb("ps_t"), pb("ps_z")
        ps_c, ps_a, ps_d = ([pb(f"ps_{k}{b}") for b in range(2)] for k in "cad")
        idx_in = [sem(f"idx_in{s}") for s in range(SL)]
        gathered = [sem(f"gathered{s}") for s in range(XS)]
        landed, xg_free, pool_turn, steps, key_ready, begun, rise_zero = (
            sem(k) for k in "landed xg_free pool_turn steps key_ready begun rise_zero".split())
        (s_oh, s_pick, s_score, s_off, s_masked, s_high, s_turned, s_highk, s_z, s_top, s_new, s_rise, s_max,
         s_dst, s_c, s_pre, s_sub, s_e, s_wgt, s_sum, s_scaled, s_dscaled, s_acc, s_den, s_fall) = (sem("s_" + k) for k in (
             "oh pick score off masked high turned highk z top new rise max dst c pre sub e wgt sum scaled dscaled acc den fall").split())
        row_ps, row_out, row_max, merged, den_out = (sem(k) for k in "row_ps row_out row_max merged den_out".split())
        row_banks = ps_a, ps_c, ps_d
        block = ctx.enter_context(nc.Block())

        def kv(ap):
            return ap.rearrange("p (t n) -> p t n", t=NT)

        @block.sync
        def _(sp):
            load_indices(sp, a, h, idx, idx_in, gathered, landed)
            sp.wait_ge(merged, 1)
            for t in range(NT):
                sp.dma_start(den[:, t, :], state[64:65, t, 0:NP].rearrange("o (p c) -> o p c", p=P)).then_inc(den_out, 16)
            sp.wait_ge(den_out, 16 * NT)

        @block.gpsimd
        def _(pool):
            gather_units(pool, h, table, xg, ROW, idx, idx_in, gathered, xg_free, pool_turn)

        @block.scalar
        def _(act):
            act.sem_inc(row_out, NT)
            with act.Fori(0, GROUPS) as g:
                for t in range(NT):
                    act.wait_ge(row_ps, g * NT + t + 1)
                    for k in range(2):
                        last = nc.scalar.copy(state[0:64, t, bass.ds(g * GN + k * (GN // 2), GN // 2)], row_banks[t][k][0:64, 0:GN // 2])
                    last.then_inc(row_out, 1)
            with act.Fori(0, pass_count(act, h)) as r:
                def exps(n, s):
                    b = s % 2
                    act.wait_ge(s_sub, n)
                    for c in range(CH):
                        nc.scalar.activation(by_chunk[b][:, c, :], by_chunk[b][:, c, :], ACT.Exp, bias=sc2[:, b, c:c + 1])
                    act.wait_ge(s_fall, n)
                    nc.scalar.activation(rescale[:, b, :], ps_d[b][:, KEYS:2 * KEYS], ACT.Exp).then_inc(s_e, 1)

                def turn(i, first):
                    for s in range(SL):
                        n, b = (r * TURNS + i) * SL + s + 1, s % 2
                        if not (first and s < 1):
                            exps(n - 1, (s - 1) % SL)
                        if not (first and s < 2):
                            act.wait_ge(s_sum, n - 2)
                        act.wait_ge(s_dst, n)
                        act.wait_ge(s_score, n)
                        for c in range(CH):
                            last = nc.scalar.activation(by_chunk[b][:, c, :], ps_c[b][:, 0:KEYS], ACT.Relu, bias=sc[:, b, c:c + 1])
                        last.then_inc(s_pre, 1)
                turns(act, turn)
                exps((r + 1) * NU, SL - 1)

        @block.tensor
        def _(pe):
            pe.sem_inc(xg_free, XS)
            with pe.Fori(0, GROUPS) as g:
                for t in range(NT):
                    pe.wait_ge(row_out, g * NT + t + 1)
                    for k in range(2):
                        last = nc.tensor.matmul(row_banks[t][k][0:64, 0:GN // 2], h.rows_w[:, t, :],
                                                acc[:, t, bass.ds(g * GN + k * (GN // 2), GN // 2)], start=True, stop=True)
                    last.then_inc(row_ps, 1)
            pe.wait_ge(row_out, NT * GROUPS + NT)
            pe.wait_ge(row_max, GROUPS)
            pe.wait_ge(rise_zero, 1)
            with pe.Fori(0, pass_count(pe, h)) as r:
                def sums(n, s, chunks):
                    b = s % 2
                    for c in chunks:
                        last = nc.tensor.matmul(ps_a[b][:, 0:KEYS], xg[:, s % XS, c, 0:D], by_chunk[b][:, c, :], start=(c == 0), stop=(c == CH - 1))
                    if CH - 1 in chunks:
                        last.then_inc(xg_free, 1)
                        for c in range(CH):
                            last = nc.tensor.matmul(ps_d[b][64:65, 0:KEYS], h.ones[:, 0:1], by_chunk[b][:, c, :], start=(c == 0), stop=(c == CH - 1))
                        last.then_inc(s_sum, 1)

                def turn(i, first):
                    base = bases(nc, mybir.EngineType.PE, h, i * SL, SL)
                    for s in range(SL):
                        n, b = (r * TURNS + i) * SL + s + 1, s % 2
                        lag1 = not (first and s < 1)
                        pe.wait_ge(s_high, n)
                        nc.tensor.transpose(ps_t[0:KEYS, 0:P], high[:, :], h.ident).then_inc(s_turned, 1)
                        nc.tensor.matmul(kv(ps_c[b][:, 0:KEYS]), h.ones[0:1, :], state[0:1, :, bass.ds(base[s], W)], start=True, stop=True)
                        nc.tensor.matmul(kv(ps_c[b][:, KEYS:2 * KEYS]), h.slope[0:1, :], state[0:1, :, bass.ds(base[s], W)], start=True, stop=False).then_inc(s_dst, 1)
                        pe.wait_ge(s_highk, n)
                        nc.tensor.matmul(ps_z[0:65, 0:KEYS], high_k[:, :].to_broadcast([KEYS, 65]), h.ident[0:KEYS, 0:KEYS], start=True, stop=False)
                        nc.tensor.matmul(kv(ps_z[0:65, 0:KEYS]), h.ones[0:1, 0:65], state[0:1, :, bass.ds(base[s], W)], start=False, stop=True).then_inc(s_z, 1)
                        if lag1:
                            pe.wait_ge(s_wgt, n - 1)
                            sums(n - 1, (s - 1) % SL, range(0, CH // 2))
                        pe.wait_ge(s_pre, n)
                        pe.wait_ge(s_rise, n)
                        nc.tensor.matmul(ps_c[b][:, KEYS:2 * KEYS], h.less_row32[0:64, :], rise[:, 0, :], start=False, stop=True).then_inc(s_c, 1)
                        nc.tensor.matmul(ps_d[b][:, KEYS:2 * KEYS], h.less_row32[0:64, :], rise[:, 1, :], start=True, stop=True).then_inc(s_fall, 1)
                        if lag1:
                            sums(n - 1, (s - 1) % SL, range(CH // 2, CH))
                pe.wait_ge(key_ready, r + 1)
                pe.sem_inc(begun, 1)
                turns(pe, turn)
                pe.wait_ge(s_wgt, (r + 1) * NU)
                sums((r + 1) * NU, SL - 1, range(CH))

        @block.vector
        def _(dve):
            nc.vector.memset(rise[:, :, :], 0.0).then_inc(rise_zero, 1)
            with dve.Fori(0, pass_count(dve, h)) as r:
                def look_up(n, s, i, unit, part):
                    b = s % 2
                    if part == "off":
                        keys = h.key[:, bass.ds(unit, 1), :].rearrange("p o c -> p (o c)")
                        nc.vector.tensor_tensor(off[:, s % 3, :, :], h.iota.unsqueeze(1).to_broadcast([P, CH, KEYS]),
                                                keys.unsqueeze(2).to_broadcast([P, CH, KEYS]), ALU.not_equal).then_inc(s_off, 1)
                    elif part == "type":
                        types = typ[:, bass.ds(unit, 1), :].rearrange("p o c -> p (o c)")
                        nc.vector.tensor_tensor(oh3[:, :, :], types.unsqueeze(2).to_broadcast([P, CH, NT]),
                                                h.iota[:, 0:NT].unsqueeze(1).to_broadcast([P, CH, NT]), ALU.is_equal).then_inc(s_oh, 1)
                    elif part == "pick":
                        dve.wait_ge(gathered[s % XS], GI * (PER * (r * TURNS + i) + s // XS + 1))
                        dve.wait_ge(s_oh, n)
                        nc.vector.tensor_tensor(pick[:, :, :], oh3[:, :, :], xg[:, s % XS, :, D:D + NT], ALU.mult).then_inc(s_pick, 1)
                    elif part == "score":
                        dve.wait_ge(s_pick, n)
                        nc.vector.tensor_reduce(out=sc[:, b, :], in_=pick[:, :, :], op=ALU.add, axis=AX.X).then_inc(s_score, 1)
                    else:
                        dve.wait_ge(s_score, n)
                        nc.vector.tensor_scalar(sc2[:, b, :], sc[:, b, :], SLOPE, None, ALU.mult)

                def mask(n, s):
                    dve.wait_ge(s_off, n)
                    dve.wait_ge(s_score, n)
                    nc.vector.scalar_tensor_tensor(out=masked, in0=off[:, s % 3, :, :], scalar=-BIG,
                                                   in1=sc[:, s % 2, :].unsqueeze(2).to_broadcast([P, CH, KEYS]), op0=ALU.mult, op1=ALU.add).then_inc(s_masked, 1)

                def highest(n):
                    dve.wait_ge(s_masked, n)
                    nc.vector.tensor_reduce(out=high[:, :], in_=masked.rearrange("p c k -> p k c"), op=ALU.max, axis=AX.X).then_inc(s_high, 1)

                def highest_key(n):
                    dve.wait_ge(s_turned, n)
                    nc.vector.tensor_reduce(out=high_k[:, :], in_=ps_t[0:KEYS, 0:P], op=ALU.max, axis=AX.X).then_inc(s_highk, 1)

                def raise_max(n, base, part, fresh):
                    m = state[32:33, :, bass.ds(base, W)]
                    if part == 0:
                        if not fresh:
                            dve.wait_ge(s_max, n - 1)
                        dve.wait_ge(s_z, n)
                        nc.vector.tensor_tensor(kv(top[32:33, :]), kv(ps_z[32:33, 0:KEYS]), m, ALU.max).then_inc(s_top, 1)
                    elif part == 1:
                        dve.wait_ge(s_top, n)
                        nc.vector.scalar_tensor_tensor(out=rise[32:33, 0, :], in0=ps_z[32:33, 0:KEYS], scalar=SLOPE, in1=top[32:33, :],
                                                       op0=ALU.mult, op1=ALU.max).then_inc(s_new, 1)
                    elif part == 2:
                        dve.wait_ge(s_new, n)
                        nc.vector.tensor_tensor(kv(rise[32:33, 1, :]), kv(rise[32:33, 0, :]), m, ALU.subtract).then_inc(s_rise, 1)
                    else:
                        dve.wait_ge(s_rise, n)
                        nc.vector.tensor_tensor(m, m, kv(rise[32:33, 0, :]), ALU.max).then_inc(s_max, 1)

                def less_max(n, s):
                    b = s % 2
                    dve.wait_ge(s_pre, n)
                    dve.wait_ge(s_c, n)
                    nc.vector.scalar_tensor_tensor(out=by_chunk[b], in0=by_chunk[b], scalar=1.0 - SLOPE,
                                                   in1=ps_c[b][:, KEYS:2 * KEYS].unsqueeze(1).to_broadcast([P, CH, KEYS]),
                                                   op0=ALU.mult, op1=ALU.add).then_inc(s_sub, 1)

                def weights(n, s):
                    b = s % 2
                    dve.wait_ge(s_e, n)
                    nc.vector.scalar_tensor_tensor(out=e[:, b, :], in0=off[:, s % 3, :, :].rearrange("p c k -> p (c k)"), scalar=0.0,
                                                   in1=e[:, b, :], op0=ALU.is_equal, op1=ALU.min).then_inc(s_wgt, 1)

                def scale_sums(n, s, base, fresh):
                    win = bass.ds(base, W)
                    if not fresh:
                        dve.wait_ge(s_acc, n - 1)
                    nc.vector.tensor_tensor(acc[:, :, win], acc[:, :, win], kv(rescale[:, s % 2, :]), ALU.mult).then_inc(s_scaled, 1)

                def scale_denominators(n, s, base, fresh):
                    win = bass.ds(base, W)
                    if not fresh:
                        dve.wait_ge(s_den, n - 1)
                    nc.vector.tensor_tensor(state[64:65, :, win], state[64:65, :, win], kv(rescale[64:65, s % 2, :]), ALU.mult).then_inc(s_dscaled, 1)

                def add_sums(n, s, base):
                    b = s % 2
                    win = bass.ds(base, W)
                    dve.wait_ge(s_scaled, n)
                    dve.wait_ge(s_sum, n)
                    nc.vector.tensor_tensor(acc[:, :, win], acc[:, :, win], kv(ps_a[b][:, 0:KEYS]), ALU.add).then_inc(s_acc, 1)
                    dve.wait_ge(s_dscaled, n)
                    nc.vector.tensor_tensor(state[64:65, :, win], state[64:65, :, win], kv(ps_d[b][64:65, 0:KEYS]), ALU.add).then_inc(s_den, 1)

                def step(n, s, i, unit, base, stages, fresh):
                    look, chain, weigh, merge = (k in stages for k in range(4))
                    if chain:
                        mask(n - 1, s - 1)
                    if weigh:
                        less_max(n - 2, s - 2)
                    if chain:
                        highest(n - 1)
                    if look:
                        look_up(n, s, i, unit, "off")
                    if chain:
                        highest_key(n - 1)
                    if merge:
                        add_sums(n - 3, s - 3, base(3))
                    if look:
                        look_up(n, s, i, unit, "type")
                    if weigh:
                        weights(n - 2, s - 2)
                    if look:
                        look_up(n, s, i, unit, "pick")
                    if chain:
                        raise_max(n - 1, base(1), 0, fresh and s == 1)
                    if weigh:
                        scale_sums(n - 2, s - 2, base(2), fresh and s == 2)
                    if chain:
                        raise_max(n - 1, base(1), 1, False)
                    if look:
                        look_up(n, s, i, unit, "score")
                    if chain:
                        raise_max(n - 1, base(1), 2, False)
                    if weigh:
                        scale_denominators(n - 2, s - 2, base(2), fresh and s == 2)
                    if chain:
                        raise_max(n - 1, base(1), 3, False)
                    if look:
                        look_up(n, s, i, unit, "twice")

                def turn(i, first):
                    back = 0 if first else 3
                    base = bases(nc, mybir.EngineType.DVE, h, i * SL - back, SL - 1 + back)
                    for s in range(SL):
                        step((r * TURNS + i) * SL + s + 1, s, i, i * SL + s, lambda k: base[s + back - k],
                             [k for k in range(4) if not first or k <= s], first)

                start_pass(nc, dve, h, r, steps, key_ready, begun, rel, typ)
                with dve.If(r < 1), dve.Fori(0, GROUPS) as g:
                    dve.wait_ge(row_out, NT * g + 2 * NT)
                    own = state[32:33, :, bass.ds(g * GN, GN)]
                    nc.vector.scalar_tensor_tensor(out=own, in0=own, scalar=SLOPE, in1=own, op0=ALU.mult, op1=ALU.max).then_inc(row_max, 1)
                turns(dve, turn)
                base = bases(nc, mybir.EngineType.DVE, h, NU - 3, 3)
                for s in range(3):
                    step((r + 1) * NU + s + 1, s, None, None, lambda k: base[s + 3 - k], range(s + 1, 4), False)
                dve.wait_ge(s_acc, (r + 1) * NU)
                dve.wait_ge(s_den, (r + 1) * NU)
            dve.sem_inc(merged, 1)


def finish_attention(nc, h, a, acc, den, rden, table, y):
    with ExitStack() as ctx:
        sb = lambda name, shape, dt=fp32: ctx.enter_context(nc.sbuf_tensor("fa_" + name, shape, dt))
        pb = lambda name: ctx.enter_context(nc.psum_tensor("fa_" + name, [P, 1024], fp32))
        sem = lambda name: ctx.enter_context(nc.semaphore("fa_" + name))
        r = sb("r", [P, NT, NP // P])
        w, bias, dw, db = sb("w", [P, NT, D]), sb("bias", [NT, D]), sb("dw", [P, D]), sb("db", [P, D])
        inv_den, att = sb("inv_den", [P, 2, NT, GN]), sb("att_sum", [P, 2, NT, GN])
        x, relu, hd = sb("x", [P, 2, G, D]), sb("relu", [P, G, D]), sb("hd", [P, G, D])
        stats, moments = sb("stats", [P, G, 6]), sb("moments", [P, G, 2])
        dev, inv, shift, eps = sb("dev", [P, G]), sb("inv", [P, G]), sb("shift", [P, G]), sb("eps", [P, 1])
        ht = sb("ht", [P, GN])
        ps_o, ps_h, ps_m = pb("ps_o"), pb("ps_h"), pb("ps_m")
        x_in, d_in = ([sem(f"{k}{s}") for s in range(2)] for k in ("x_in", "d_in"))
        (s_inverted, rden_out, w_in, t_done, t_free, epsilon, s_att, s_out, s_x1, s_stats, s_begun, s_var,
         s_dev, s_inv, s_shift, s_relu, s_y, s_turned, s_ht, s_hd, s_hdc) = (sem(k) for k in (
             "inverted rden_out w_in t_done t_free eps att out x1 stats begun var dev inv shift relu y "
             "turned ht hd hdc").split())
        block = ctx.enter_context(nc.Block())

        @block.sync
        def _(sp):
            def load_den(g, s):
                sp.dma_start(inv_den[:, s, :, :], rden[:, bass.ds(g * GN, GN)].rearrange("(o t) n -> o t n", o=1).to_broadcast([P, NT, GN])).then_inc(d_in[s], 16)

            def load_x(g):
                if g > 1:
                    sp.wait_ge(s_y, g - 1)
                sp.dma_start(x[:, g % 2, :, :], a["x"][g, :, :, :]).then_inc(x_in[g % 2], 16)

            sp.dma_start(w[:, :, :], a["L0_gnn_W"].rearrange("t i o -> i t o")).then_inc(w_in, 16)
            sp.dma_start(bias[:, :], a["L0_gnn_bias"][:, :]).then_inc(w_in, 16)
            load_x(0)
            sp.dma_start(dw[:, :], a["L1_gnn_dW"][:, :]).then_inc(w_in, 16)
            sp.dma_start(db[:, :], a["L1_gnn_db"].rearrange("(o f) -> o f", o=1).to_broadcast([P, D])).then_inc(w_in, 16)
            load_x(1)
            sp.wait_ge(s_inverted, 1)
            sp.dma_start(rden.rearrange("t (p c) -> p t c", p=P), r[:, :, :]).then_inc(rden_out, 16)
            sp.wait_ge(rden_out, 16)
            for g in range(2):
                load_den(g, g)
            for g in range(2, GROUPS):
                sp.wait_ge(s_att, g - 1)
                load_den(g, g % 2)
                if g > 2:
                    load_x(g - 1)
            load_x(GROUPS - 1)

        @block.gpsimd
        def _(pool):
            pool.sem_inc(t_free, 1)
            with pool.Fori(0, GROUPS) as g:
                pool.wait_ge(s_hdc, g + 1)
                pool.dma_start(table[bass.ds(g * GN, GN), :].rearrange("(t p) r -> p t r", p=P), hd[:, :, :]).then_inc(t_done, 16)
                pool.wait_ge(t_done, 16 * g + 16)
                pool.sem_inc(t_free, 1)

        @block.tensor
        def _(pe):
            def project(g, s):
                pe.wait_ge(s_att, g + 1)
                for j in range(G):
                    for t in range(NT):
                        nc.tensor.matmul(ps_o[:, j * P:(j + 1) * P], att[:, s, t, j * P:(j + 1) * P], w[:, t, :], start=(t == 0), stop=False)
                    last = nc.tensor.matmul(ps_o[:, j * P:(j + 1) * P], h.ones[0:NT, :], bias[:, :], start=False, stop=True)
                last.then_inc(s_out, 1)

            def turn(g):
                pe.wait_ge(s_relu, g + 1)
                for j in range(G):
                    last = nc.tensor.transpose(ps_h[:, j * P:(j + 1) * P], relu[:, j, :], h.ident)
                last.then_inc(s_turned, 1)

            def messages(g, first):
                pe.wait_ge(s_ht, g + 1)
                if not first:
                    pe.wait_ge(s_hdc, g)
                for j in range(G):
                    last = nc.tensor.matmul(ps_m[:, j * P:(j + 1) * P], ht[:, j * P:(j + 1) * P], dw[:, :], start=True, stop=True)
                last.then_inc(s_hd, 1)

            def group(g, s, first):
                pe.wait_ge(s_x1, g + 1)
                project(g + 1, 1 - s)
                turn(g)
                messages(g, first)

            pe.wait_ge(w_in, 64)
            project(0, 0)
            group(0, 0, True)
            with pe.Fori(0, (GROUPS - 3) // 2) as i:
                group(2 * i + 1, 1, False)
                group(2 * i + 2, 0, False)
            group(GROUPS - 2, 1, False)
            turn(GROUPS - 1)
            messages(GROUPS - 1, False)

        @block.scalar
        def _(act):
            def group(g, s, first):
                act.wait_ge(s_var, g + 1)
                nc.scalar.activation(dev[:, :], moments[:, :, 1], ACT.Sqrt, bias=eps[:, :]).then_inc(s_dev, 1)
                act.wait_ge(s_shift, g + 1)
                if not first:
                    act.wait_ge(s_y, g)
                for j in range(G):
                    last = nc.scalar.activation(relu[:, j, :], x[:, s, j, :], ACT.Relu, bias=shift[:, j:j + 1], scale=inv[:, j:j + 1])
                last.then_inc(s_relu, 1)
                act.wait_ge(s_turned, g + 1)
                if not first:
                    act.wait_ge(s_hd, g)
                nc.scalar.copy(ht[:, :], ps_h[:, 0:GN]).then_inc(s_ht, 1)
            act.wait_ge(epsilon, 1)
            node_groups(group)(act)

        @block.vector
        def _(dve):
            def normalise_sums(g, s, count):
                dve.wait_ge(d_in[s], 16 * count + 16)
                nc.vector.tensor_tensor(att[:, s, :, :], acc[:, :, bass.ds(g * GN, GN)], inv_den[:, s, :, :], ALU.mult).then_inc(s_att, 1)

            def store_messages(g):
                dve.wait_ge(s_hd, g + 1)
                dve.wait_ge(t_free, g + 1)
                nc.vector.tensor_tensor(hd[:, :, :], ps_m[:, 0:GN].rearrange("p (t f) -> p t f", t=G),
                                        db[:, :].unsqueeze(1).to_broadcast([P, G, D]), ALU.add).then_inc(s_hdc, 1)

            def group(g, s, count, first, ahead):
                dve.wait_ge(x_in[s], 16 * count + 16)
                dve.wait_ge(s_out, g + 1)
                xf = x[:, s, :, :].rearrange("p t f -> p (t f)")
                nc.vector.tensor_tensor(xf, xf, ps_o[:, 0:GN], ALU.add).then_inc(s_x1, 1)
                dve.wait_ge(s_x1, g + 1)
                for j in range(G):
                    last = nc.vector.bn_stats(stats[:, j, :], x[:, s, j, :])
                last.then_inc(s_stats, 1)
                dve.wait_ge(s_stats, g + 1)
                dve.sem_inc(s_begun, 1)
                for j in range(G):
                    last = nc.vector.bn_aggr(moments[:, j, :], stats[:, j, :])
                last.then_inc(s_var, 1)
                if not first:
                    store_messages(g - 1)
                dve.wait_ge(s_dev, g + 1)
                nc.vector.reciprocal(inv[:, :], dev[:, :]).then_inc(s_inv, 1)
                dve.wait_ge(s_inv, g + 1)
                nc.vector.scalar_tensor_tensor(out=shift[:, :], in0=moments[:, :, 0], scalar=-1.0, in1=inv[:, :],
                                               op0=ALU.mult, op1=ALU.mult).then_inc(s_shift, 1)
                if ahead:
                    normalise_sums(g + 2, s, count + 1)
                dve.wait_ge(s_relu, g + 1)
                nc.vector.tensor_tensor(y[:, bass.ds(g, 1), :, :].rearrange("p o t f -> p (o t) f"), x[:, s, :, :], relu[:, :, :], ALU.add).then_inc(s_y, 1)

            nc.vector.memset(eps[:, :], EPS).then_inc(epsilon, 1)
            nc.vector.reciprocal(r[:, :, :], den[:, :, :]).then_inc(s_inverted, 1)
            dve.wait_ge(w_in, 64)
            normalise_sums(0, 0, 0)
            normalise_sums(1, 1, 0)
            group(0, 0, 0, True, True)
            with dve.Fori(0, (GROUPS - 3) // 2) as i:
                group(2 * i + 1, 1, i, False, True)
                group(2 * i + 2, 0, i + 1, False, True)
            group(GROUPS - 2, 1, (GROUPS - 2) // 2, False, False)
            group(GROUPS - 1, 0, (GROUPS - 1) // 2, False, False)
            store_messages(GROUPS - 1)


def convolution_edges(nc, h, a, acc, update, table):
    with ExitStack() as ctx:
        sb = lambda name, shape, dt=fp32: ctx.enter_context(nc.sbuf_tensor("ce_" + name, shape, dt))
        pb = lambda name, n=1024: ctx.enter_context(nc.psum_tensor("ce_" + name, [P, n], fp32))
        sem = lambda name: ctx.enter_context(nc.semaphore("ce_" + name))
        H = UE // 2
        fw1, fb1, fw2, fb2 = sb("fw1", [RBF, D]), sb("fb1", [D, 1]), sb("fw2", [D, D]), sb("fb2", [P, D])
        idx = [sb(f"idx{s}", [P, CH], i32) for s in range(SL)]
        xg = sb("xg", [P, XS, CH, D])
        ea = sb("ea", [RBF, XS, UE])
        hid = sb("hid", [P, 2, UE])
        msg = sb("msg", [P, 3, CH, D])
        hot = sb("hot", [P, 3, CH, W])
        rel = sb("rel", [P, NU, CH])
        ps_h = pb("ps_h")
        ps_f = [pb(f"ps_f{b}") for b in range(2)]
        ps_a = [pb(f"ps_a{b}", 512) for b in range(2)]
        idx_in = [sem(f"idx_in{s}") for s in range(SL)]
        sem_landed = sem("landed")
        gathered = [sem(f"gathered{s}") for s in range(XS)]
        ea_in = [sem(f"ea_in{s}") for s in range(XS)]
        (w_in, xg_free, pool_turn, ea_free, steps, key_ready, begun, cleared, s_hid, s_act, s_flt, s_bias, s_hot, s_msg, s_sum, s_acc) = (
            sem("c_" + k) for k in "w_in xg_free pool_turn ea_free steps key_ready begun cleared hid act flt bias hot msg sum acc".split())
        block = ctx.enter_context(nc.Block())

        @block.sync
        def _(sp):
            def weights():
                sp.dma_start(fw1[:, :], a["L1_gnn_fW1"][:, :]).then_inc(w_in, 16)
                sp.dma_start(fb1[:, :], a["L1_gnn_fb1"].rearrange("(f o) -> f o", o=1)).then_inc(w_in, 16)
                sp.dma_start(fw2[:, :], a["L1_gnn_fW2"][:, :]).then_inc(w_in, 16)
                sp.dma_start(fb2[:, :], a["L1_gnn_fb2"].rearrange("(o f) -> o f", o=1).to_broadcast([P, D])).then_inc(w_in, 16)
                update.load(sp, a)

            def attributes(r, i, s):
                n = (r * TURNS + i) * SL + s + 1
                sp.wait_ge(s_hid, n)
                sp.dma_start(ea[:, s % XS, :], a["edge_attr_50"][:, bass.ds((i * SL + s) * UE, UE)]).then_inc(ea_in[s % XS], 16)
            load_indices(sp, a, h, idx, idx_in, gathered, sem_landed, attributes, weights)

        @block.scalar
        def _(act):
            act.wait_ge(w_in, 64)
            with act.Fori(0, pass_count(act, h)) as r:
                def turn(i, first):
                    for s in range(SL):
                        n, b = (r * TURNS + i) * SL + s + 1, s % 2
                        act.wait_ge(s_hid, n + XS)
                        if not (first and s < 2):
                            act.wait_ge(s_flt, n - 2)
                        nc.scalar.activation(hid[:, b, :].rearrange("p (k e) -> p k e", k=2), ps_h[:, :].rearrange("p (k e) -> p k e", k=2)[:, :, 0:H],
                                             ACT.Silu, bias=fb1[:, :]).then_inc(s_act, 1)
                turns(act, turn)

        @block.gpsimd
        def _(pool):
            gather_units(pool, h, table, xg, D, idx, idx_in, gathered, s_msg, pool_turn)

        @block.tensor
        def _(pe):
            pe.sem_inc(s_hid, XS)
            pe.wait_ge(w_in, 64)
            with pe.Fori(0, pass_count(pe, h)) as r:
                def filters(n, s, fresh):
                    b = s % 2
                    pe.wait_ge(s_act, n)
                    if not fresh:
                        pe.wait_ge(s_bias, n - 2)
                    for c in range(CH):
                        last = nc.tensor.matmul(ps_f[b][:, c * D:(c + 1) * D], hid[:, b, c * P:(c + 1) * P], fw2[:, :], start=True, stop=True)
                    last.then_inc(s_flt, 1)

                def sums(n, s, fresh):
                    if not fresh:
                        pe.wait_ge(s_acc, n - 2)
                    pe.wait_ge(s_msg, n + XS)
                    for c in range(CH):
                        last = nc.tensor.matmul(ps_a[s % 2][:, 0:W], msg[:, s % 3, c, :], hot[:, s % 3, c, :], start=(c == 0), stop=(c == CH - 1))
                    last.then_inc(s_sum, 1)

                def turn(i, first):
                    for s in range(SL):
                        n = (r * TURNS + i) * SL + s + 1
                        if not (first and s < 1):
                            pe.wait_ge(s_act, n - 1)
                        pe.wait_ge(ea_in[s % XS], 16 * (PER * (r * TURNS + i) + s // XS + 1))
                        for k in range(2):
                            last = nc.tensor.matmul(ps_h[:, k * 512:k * 512 + H], fw1[:, :], ea[:, s % XS, k * H:(k + 1) * H], start=True, stop=True)
                        last.then_inc(s_hid, 1)
                        if not (first and s < 1):
                            filters(n - 1, (s - 1) % SL, first and s < 3)
                        if not (first and s < 3):
                            sums(n - 3, (s - 3) % SL, first and s < 5)
                turns(pe, turn)
                n = (r + 1) * NU
                filters(n, SL - 1, False)
                for s in range(3):
                    sums(n - 2 + s, SL - 3 + s, False)

        @block.vector
        def _(dve):
            dve.sem_inc(s_msg, XS)
            nc.vector.memset(h.sweep[:, :], 0.0).then_inc(cleared, 1)
            nc.vector.memset(acc[:, :], 0.0).then_inc(cleared, 1)
            dve.wait_ge(cleared, 2)
            dve.wait_ge(w_in, 64)
            with dve.Fori(0, pass_count(dve, h)) as r:
                def one_hot(unit, s):
                    keys = h.key[:, bass.ds(unit, 1), :].rearrange("p o c -> p (o c)")
                    nc.vector.tensor_tensor(hot[:, s % 3, :, :], h.iota[:, 0:W].unsqueeze(1).to_broadcast([P, CH, W]),
                                            keys.unsqueeze(2).to_broadcast([P, CH, W]), ALU.is_equal).then_inc(s_hot, 1)

                def messages(n, s, count):
                    dve.wait_ge(s_flt, n)
                    nc.vector.tensor_tensor(msg[:, s % 3, :, :], ps_f[s % 2][:, 0:CH * D].rearrange("p (c f) -> p c f", c=CH),
                                            fb2[:, :].unsqueeze(1).to_broadcast([P, CH, D]), ALU.add).then_inc(s_bias, 1)
                    dve.wait_ge(s_bias, n)
                    dve.wait_ge(gathered[s % XS], GI * count)
                    nc.vector.tensor_tensor(msg[:, s % 3, :, :], msg[:, s % 3, :, :], xg[:, s % XS, :, :], ALU.mult).then_inc(s_msg, 1)

                def merge(n, s, base, fresh):
                    dve.wait_ge(s_sum, n)
                    if not fresh:
                        dve.wait_ge(s_acc, n - 1)
                    win = bass.ds(base, W)
                    nc.vector.tensor_tensor(acc[:, win], acc[:, win], ps_a[s % 2][:, 0:W], ALU.add).then_inc(s_acc, 1)

                def turn(i, first):
                    back = 0 if first else 4
                    base = bases(nc, mybir.EngineType.DVE, h, i * SL - back, SL - 4 + back)
                    for s in range(SL):
                        t = r * TURNS + i
                        n, v = t * SL + s + 1, (s - 1) % SL
                        if not (first and s < 4):
                            merge(n - 4, (s - 4) % SL, base[s + back - 4], first and s == 4)
                        if not (first and s < 1):
                            one_hot(i * SL + s - 1, v)
                            messages(n - 1, v, PER * t + v // XS + 1 - (PER if s == 0 else 0))

                start_pass(nc, dve, h, r, steps, key_ready, begun, rel[:, :, :])
                turns(dve, turn)
                n = (r + 1) * NU
                base = bases(nc, mybir.EngineType.DVE, h, NU - 4, 4)
                merge(n - 3, SL - 4, base[0], False)
                one_hot(NU - 1, SL - 1)
                messages(n, SL - 1, PER * TURNS * (r + 1))
                for s in range(1, 4):
                    merge(n - 3 + s, SL - 4 + s, base[s], False)
                dve.wait_ge(s_acc, n)


class Update:

    def __init__(self, nc, ctx):
        sb = lambda name, shape: ctx.enter_context(nc.sbuf_tensor("up_" + name, shape, fp32))
        self.w1, self.b1, self.w2, self.b2 = sb("w1", [D, D]), sb("b1", [D, 1]), sb("w2", [D, D]), sb("b2", [P, D])
        self.loaded = ctx.enter_context(nc.semaphore("up_loaded"))

    def load(self, sp, a):
        sp.dma_start(self.w1[:, :], a["L1_gnn_uW1"][:, :]).then_inc(self.loaded, 16)
        sp.dma_start(self.b1[:, :], a["L1_gnn_ub1"].rearrange("(f o) -> f o", o=1)).then_inc(self.loaded, 16)
        sp.dma_start(self.w2[:, :], a["L1_gnn_uW2"][:, :]).then_inc(self.loaded, 16)
        sp.dma_start(self.b2[:, :], a["L1_gnn_ub2"].rearrange("(o f) -> o f", o=1).to_broadcast([P, D])).then_inc(self.loaded, 16)


def finish(nc, h, acc, update, y, out):
    with ExitStack() as ctx:
        sb = lambda name, shape, dt=fp32: ctx.enter_context(nc.sbuf_tensor("fi_" + name, shape, dt))
        pb = lambda name: ctx.enter_context(nc.psum_tensor("fi_" + name, [P, 1024], fp32))
        sem = lambda name: ctx.enter_context(nc.semaphore("fi_" + name))
        hid = sb("hid", [P, 2, GN])
        ps_u, ps_y = [pb(f"ps_u{s}") for s in range(2)], [pb(f"ps_y{s}") for s in range(2)]
        (out_done, s_u, s_hid, s_v, s_bias, s_y) = (sem(k) for k in "out_done u hid v bias y".split())
        half = GN // 2
        block = ctx.enter_context(nc.Block())

        @block.sync
        def _(sp):
            with sp.Fori(0, GROUPS) as g:
                sp.wait_ge(s_y, g + 1)
                sp.dma_start(out[bass.ds(g * GN, GN), :].rearrange("(t p) f -> p t f", p=P),
                             y[:, bass.ds(g, 1), :, :].rearrange("p o t f -> p (o t) f")).then_inc(out_done, 16)
            sp.wait_ge(out_done, 16 * GROUPS)

        @block.tensor
        def _(pe):
            def first_product(g, s):
                for k in range(2):
                    last = nc.tensor.matmul(ps_u[s][:, k * 512:k * 512 + half], update.w1[:, :],
                                            acc[:, bass.ds(g * GN + k * half, half)], start=True, stop=True)
                last.then_inc(s_u, 1)

            def second_product(g, s, fresh):
                pe.wait_ge(s_hid, g + 1)
                if not fresh:
                    pe.wait_ge(s_y, g - 1)
                for j in range(G):
                    last = nc.tensor.matmul(ps_y[s][:, j * P:(j + 1) * P], hid[:, s, j * P:(j + 1) * P], update.w2[:, :], start=True, stop=True)
                last.then_inc(s_v, 1)

            pe.wait_ge(update.loaded, 64)
            first_product(0, 0)
            for g in range(2):
                first_product(g + 1, 1 - g)
                second_product(g, g, True)
            with pe.Fori(0, (GROUPS - 3) // 2) as i:
                for s in range(2):
                    first_product(2 * i + s + 3, 1 - s)
                    second_product(2 * i + s + 2, s, False)
            second_product(GROUPS - 1, 0, False)

        @block.scalar
        def _(act):
            act.wait_ge(update.loaded, 64)

            def hidden(g, s, fresh):
                act.wait_ge(s_u, g + 1)
                if not fresh:
                    act.wait_ge(s_v, g - 1)
                nc.scalar.activation(hid[:, s, :].rearrange("p (k n) -> p k n", k=2), ps_u[s][:, :].rearrange("p (k n) -> p k n", k=2)[:, :, 0:half],
                                     ACT.Silu, bias=update.b1[:, :]).then_inc(s_hid, 1)
            hidden(0, 0, True)
            hidden(1, 1, True)
            with act.Fori(0, (GROUPS - 3) // 2) as i:
                hidden(2 * i + 2, 0, False)
                hidden(2 * i + 3, 1, False)
            hidden(GROUPS - 1, 0, False)

        @block.vector
        def _(dve):
            dve.wait_ge(update.loaded, 64)

            def add_bias(g):
                of = y[:, bass.ds(g, 1), :, :].rearrange("p o t f -> p (o t) f")
                nc.vector.tensor_tensor(of, of, update.b2[:, :].unsqueeze(1).to_broadcast([P, G, D]), ALU.add).then_inc(s_bias, 1)

            def add_update(g, s):
                dve.wait_ge(s_v, g + 1)
                dve.wait_ge(s_bias, g + 1)
                of = y[:, bass.ds(g, 1), :, :].rearrange("p o t f -> p (o t f)")
                nc.vector.tensor_tensor(of, of, ps_y[s][:, 0:GN], ALU.add).then_inc(s_y, 1)

            add_bias(0)
            with dve.Fori(0, (GROUPS - 1) // 2) as i:
                for s in range(2):
                    add_bias(2 * i + s + 1)
                    add_update(2 * i + s, s)
            add_update(GROUPS - 1, 0)


def program(nc, a, out):
    table0 = nc.dram_tensor("table0", (NP, ROW), fp32).ap()
    table1 = nc.dram_tensor("table1", (NP, D), fp32).ap()
    rden = nc.dram_tensor("rden", (NT, NP), fp32).ap()
    with ExitStack() as ctx:
        h = Held(nc, ctx)
        sums = ctx.enter_context(nc.sbuf_tensor("sums", [P, NT, NW], fp32))
        den = ctx.enter_context(nc.sbuf_tensor("den", [P, NT, NP // P], fp32))
        with nc.sbuf_tensor("state", [P, NT, NW], fp32) as state, nc.sbuf_tensor("typ", [P, NU, CH], bf16) as typ:
            prepare(nc, h, a, sums, state, typ, table0)
            attention_edges(nc, h, a, sums, state, typ, table0, den)
        y = ctx.enter_context(nc.sbuf_tensor("y", [P, GROUPS, G, D], fp32))
        finish_attention(nc, h, a, sums, den, rden, table1, y)
        update = Update(nc, ctx)
        messages = sums[:, 0, :]
        convolution_edges(nc, h, a, messages, update, table1)
        finish(nc, h, messages, update, y, out)


def kernel(**inputs):
    import concourse.bacc as bacc
    from concourse.bass_utils import run_bass_kernel_spmd

    def padded(v, n, fill):
        return np.concatenate([v, np.full((n - v.shape[0],) + v.shape[1:], fill, v.dtype)])

    def by_unit(v, fill):
        return padded(np.asarray(v), EP, fill).reshape(NU, CH, P).transpose(0, 2, 1)

    given = {k: np.asarray(v) for k, v in inputs.items()}
    arrays = {k: given[k] for k in (
        "L0_gnn_emb_table", "L0_gnn_W", "L0_gnn_bias", "L1_gnn_fW1", "L1_gnn_fb1", "L1_gnn_fW2", "L1_gnn_fb2",
        "L1_gnn_dW", "L1_gnn_db", "L1_gnn_uW1", "L1_gnn_ub1", "L1_gnn_uW2", "L1_gnn_ub2")}
    arrays["cst"] = constants()
    arrays["x"] = padded(given["x"], NP, 0).reshape(GROUPS, G, P, D).transpose(0, 2, 1, 3)
    arrays["node_type_3"] = padded(given["node_type_3"], NP, 0).reshape(1, NP)
    arrays["src"] = by_unit(given["src"], 0)
    arrays["dst"] = by_unit(given["dst"], N).transpose(1, 0, 2)
    arrays["edge_type_3"] = by_unit(given["edge_type_3"], 0).transpose(1, 0, 2)
    arrays["edge_attr_50"] = padded(given["edge_attr_50"], EP, 0).T
    arrays["w_t"] = given["L0_gnn_W"].transpose(2, 0, 1)
    arrays["att"] = np.concatenate([given["L0_gnn_att_src"], given["L0_gnn_att_dst"]]).T

    nc = bacc.Bacc("TRN2", target_bir_lowering=False, num_devices=1)
    arrays = {"in_" + k: np.ascontiguousarray(v) for k, v in arrays.items()}
    a = {k[3:]: nc.dram_tensor(k, v.shape, mybir.dt.from_np(v.dtype), kind="ExternalInput").ap() for k, v in arrays.items()}
    out = nc.dram_tensor("out_x", (NP, D), fp32, kind="ExternalOutput").ap()
    program(nc, a, out)
    r = run_bass_kernel_spmd(nc, [arrays], core_ids=[0])
    return r.results[0]["out_x"][:N]
```
